# Optimizing a Trainium2 kernel written in Bass

```python
import numpy as np
import jax
import jax.numpy as jnp

def _softmax(x, axis=-1):
    return jax.nn.softmax(x, axis=axis)

def _gelu(x):
    return jax.nn.gelu(x, approximate=True)

def _silu(x):
    return jax.nn.silu(x)

def _sigmoid(x):
    return jax.nn.sigmoid(x)

def _layernorm(x, axis=-1, eps=1e-05):
    m = jnp.mean(x, axis=axis, keepdims=True)
    v = jnp.var(x, axis=axis, keepdims=True)
    return (x - m) / jnp.sqrt(v + eps)

def _scatter_add(tgt, idx, src, axis=0):
    return tgt.at[idx].add(src)

def _segment_sum(src, seg, n):
    return jax.ops.segment_sum(src, seg, n)
kernel_name = 'mk_adj_resnorm_d4_adj_r2_f21167'

def setup_inputs(seed: int=0):
    np.random.seed(seed)
    _w = jnp.asarray

    def _rec_inputs():
        import jax
        import jax.numpy as jnp
        _gk = jax.random.key(seed)
        x = 7.22e-05 + 1 * jax.random.normal(jax.random.fold_in(_gk, 1), (16, 512, 256), jnp.float32)
        _a = jax.random.bernoulli(jax.random.fold_in(_gk, 2), 0.015625, (16, 512, 512))
        _a = jnp.logical_or(_a, jnp.swapaxes(_a, -1, -2))
        _a = jnp.logical_or(_a, jnp.eye(512, dtype=bool))
        _af = _a.astype(jnp.float32)
        _af = _af * jax.random.uniform(jax.random.fold_in(_gk, 3), (16, 512, 512), jnp.float32, 0.05, 1)
        adj = _af
        return (x, adj)
    x, adj = _rec_inputs()

    def _L0_gnn_setup():
        import jax, jax.numpy as jnp
        import numpy as np
        EPS_LN = 1e-05

        def hypergraph_conv(x, adj, W, b):
            N, C, _ = adj.shape
            H = (adj != 0).astype(x.dtype)
            w = adj.reshape(N, -1)[:, :C]
            xw = jnp.einsum('ncd,hd->nch', x, W)
            Dn = jnp.einsum('nce,ne->nc', H, w)
            Dn = jnp.where(Dn > 0, 1.0 / Dn, 0.0)
            Be = H.sum(axis=1)
            Be = jnp.where(Be > 0, 1.0 / Be, 0.0)
            m = Be[:, :, None] * jnp.einsum('nce,nch->neh', H, xw)
            out = Dn[:, :, None] * jnp.einsum('nce,neh->nch', H, m)
            return out + b

        def layer_norm(x, g, b):
            mu = jnp.mean(x, axis=-1, keepdims=True)
            var = jnp.var(x, axis=-1, keepdims=True)
            return (x - mu) * jax.lax.rsqrt(var + EPS_LN) * g + b
        key = jax.random.key(seed)
        ks = jax.random.split(key, 4)
        N, C, Din, Dh, Dout = (16, 512, 256, 512, 256)
        x = jax.random.normal(ks[0], (N, C, Din), dtype=jnp.float32)
        adj = jax.random.uniform(ks[1], (N, C, C), dtype=jnp.float32, minval=0.1, maxval=1.0)
        W1 = jax.random.normal(ks[2], (Dh, Din), dtype=jnp.float32) * (1.0 / np.sqrt(Din))
        b1 = jnp.zeros((Dh,), dtype=jnp.float32)
        gamma = jnp.ones((Dh,), dtype=jnp.float32)
        beta = jnp.zeros((Dh,), dtype=jnp.float32)
        W2 = jax.random.normal(ks[3], (Dout, Dh), dtype=jnp.float32) * (1.0 / np.sqrt(Dh))
        b2 = jnp.zeros((Dout,), dtype=jnp.float32)
        return {'x': x, 'adj': adj, 'W1': W1, 'b1': b1, 'gamma': gamma, 'beta': beta, 'W2': W2, 'b2': b2}
    _L0_gnn_all = _L0_gnn_setup()
    _L0_gnn_in = {k: v for k, v in _L0_gnn_all.items() if k in ('W1', 'b1', 'gamma', 'beta', 'W2', 'b2')}
    del _L0_gnn_all

    def _L1_gnn_setup():
        import jax, jax.numpy as jnp
        import numpy as np
        EMBED_DIM = 256
        NUM_HEADS = 8
        HEAD_DIM = EMBED_DIM // NUM_HEADS
        SCALE = HEAD_DIM ** (-0.5)
        B, S = (16, 512)
        key = jax.random.key(seed)
        ks = jax.random.split(key, 12)
        init = lambda k, shape: jax.random.normal(k, shape, dtype=jnp.float32) * EMBED_DIM ** (-0.5)
        return {'x': jax.random.normal(ks[0], (B, S, EMBED_DIM), dtype=jnp.float32), 'adj_matrix': jax.random.uniform(ks[1], (B, S, S), dtype=jnp.float32), 'bond_matrix': jax.random.uniform(ks[2], (B, S, S), dtype=jnp.float32), 'Wq': init(ks[3], (EMBED_DIM, EMBED_DIM)), 'bq': jnp.zeros((EMBED_DIM,), jnp.float32), 'Wk': init(ks[4], (EMBED_DIM, EMBED_DIM)), 'bk': jnp.zeros((EMBED_DIM,), jnp.float32), 'Wv': init(ks[5], (EMBED_DIM, EMBED_DIM)), 'bv': jnp.zeros((EMBED_DIM,), jnp.float32), 'Wo': init(ks[6], (EMBED_DIM, EMBED_DIM)), 'bo': jnp.zeros((EMBED_DIM,), jnp.float32), 'seq_len': S}
    _L1_gnn_all = _L1_gnn_setup()
    _L1_gnn_in = {k: v for k, v in _L1_gnn_all.items() if k in ('Wq', 'bq', 'Wk', 'bk', 'Wv', 'bv', 'Wo', 'bo')}
    del _L1_gnn_all

    def _L2_gnn_setup():
        import jax, jax.numpy as jnp
        import numpy as np
        EPS = 1e-06
        key = jax.random.key(seed)
        k1, k2, k3 = jax.random.split(key, 3)
        B, N, F, O = (8, 2048, 256, 256)
        x = jax.random.normal(k1, (B, N, F), dtype=jnp.float32)
        adj = jax.random.uniform(k2, (B, N, N), dtype=jnp.float32)
        W = jax.random.normal(k3, (O, 2 * F), dtype=jnp.float32) * (1.0 / np.sqrt(2 * F))
        return {'x': x, 'adj': adj, 'W': W}
    _L2_gnn_all = _L2_gnn_setup()
    _L2_gnn_in = {k: v for k, v in _L2_gnn_all.items() if k in ('W',)}
    del _L2_gnn_all

    def _L3_gnn_setup():
        import jax, jax.numpy as jnp
        import numpy as np
        B, N, DIN, DOUT, K = (4, 1024, 256, 256, 3)
        key = jax.random.key(seed)
        ks = jax.random.split(key, 8)
        X = jax.random.normal(ks[0], (B, N, DIN), dtype=jnp.float32)
        A = jax.random.uniform(ks[1], (B, N, N), dtype=jnp.float32)
        Wv = jax.random.normal(ks[2], (DIN, DOUT), dtype=jnp.float32) * 0.02
        bv = jax.random.normal(ks[3], (DOUT,), dtype=jnp.float32) * 0.02
        aw = jax.random.normal(ks[4], (2 * DOUT, 1), dtype=jnp.float32) * 0.05
        ab = jax.random.normal(ks[5], (1,), dtype=jnp.float32) * 0.05
        Wk = jax.random.normal(ks[6], (K, DIN, DOUT), dtype=jnp.float32) * 0.02
        bk = jax.random.normal(ks[7], (K, DOUT), dtype=jnp.float32) * 0.02
        return {'X': X, 'A': A, 'Wv': Wv, 'bv': bv, 'aw': aw, 'ab': ab, 'Wk': Wk, 'bk': bk}
    _L3_gnn_all = _L3_gnn_setup()
    _L3_gnn_in = {k: v for k, v in _L3_gnn_all.items() if k in ('Wv', 'bv', 'aw', 'ab', 'Wk', 'bk')}
    del _L3_gnn_all
    return {'x': x, 'adj': adj, 'L0_gnn_W1': _L0_gnn_in['W1'], 'L0_gnn_b1': _L0_gnn_in['b1'], 'L0_gnn_gamma': _L0_gnn_in['gamma'], 'L0_gnn_beta': _L0_gnn_in['beta'], 'L0_gnn_W2': _L0_gnn_in['W2'], 'L0_gnn_b2': _L0_gnn_in['b2'], 'L1_gnn_Wq': _L1_gnn_in['Wq'], 'L1_gnn_bq': _L1_gnn_in['bq'], 'L1_gnn_Wk': _L1_gnn_in['Wk'], 'L1_gnn_bk': _L1_gnn_in['bk'], 'L1_gnn_Wv': _L1_gnn_in['Wv'], 'L1_gnn_bv': _L1_gnn_in['bv'], 'L1_gnn_Wo': _L1_gnn_in['Wo'], 'L1_gnn_bo': _L1_gnn_in['bo'], 'L2_gnn_W': _L2_gnn_in['W'], 'L3_gnn_Wv': _L3_gnn_in['Wv'], 'L3_gnn_bv': _L3_gnn_in['bv'], 'L3_gnn_aw': _L3_gnn_in['aw'], 'L3_gnn_ab': _L3_gnn_in['ab'], 'L3_gnn_Wk': _L3_gnn_in['Wk'], 'L3_gnn_bk': _L3_gnn_in['bk']}

def reference(x, adj, L0_gnn_W1, L0_gnn_b1, L0_gnn_gamma, L0_gnn_beta, L0_gnn_W2, L0_gnn_b2, L1_gnn_Wq, L1_gnn_bq, L1_gnn_Wk, L1_gnn_bk, L1_gnn_Wv, L1_gnn_bv, L1_gnn_Wo, L1_gnn_bo, L2_gnn_W, L3_gnn_Wv, L3_gnn_bv, L3_gnn_aw, L3_gnn_ab, L3_gnn_Wk, L3_gnn_bk):
    import jax
    import jax.numpy as jnp

    def _L0_gnn_ref(x, adj, W1, b1, gamma, beta, W2, b2):
        import jax, jax.numpy as jnp
        import numpy as np
        EPS_LN = 1e-05

        def hypergraph_conv(x, adj, W, b):
            N, C, _ = adj.shape
            H = (adj != 0).astype(x.dtype)
            w = adj.reshape(N, -1)[:, :C]
            xw = jnp.einsum('ncd,hd->nch', x, W)
            Dn = jnp.einsum('nce,ne->nc', H, w)
            Dn = jnp.where(Dn > 0, 1.0 / Dn, 0.0)
            Be = H.sum(axis=1)
            Be = jnp.where(Be > 0, 1.0 / Be, 0.0)
            m = Be[:, :, None] * jnp.einsum('nce,nch->neh', H, xw)
            out = Dn[:, :, None] * jnp.einsum('nce,neh->nch', H, m)
            return out + b

        def layer_norm(x, g, b):
            mu = jnp.mean(x, axis=-1, keepdims=True)
            var = jnp.var(x, axis=-1, keepdims=True)
            return (x - mu) * jax.lax.rsqrt(var + EPS_LN) * g + b
        h = jax.nn.relu(hypergraph_conv(x, adj, W1, b1))
        h = layer_norm(h, gamma, beta)
        y = hypergraph_conv(h, adj, W2, b2)
        return y + x

    def _L1_gnn_ref(x, adj_matrix, bond_matrix, Wq, bq, Wk, bk, Wv, bv, Wo, bo, seq_len):
        import jax, jax.numpy as jnp
        import numpy as np
        EMBED_DIM = 256
        NUM_HEADS = 8
        HEAD_DIM = EMBED_DIM // NUM_HEADS
        SCALE = HEAD_DIM ** (-0.5)
        B, S = (16, 512)
        b = x.shape[0]

        def proj(W, bias):
            y = jnp.einsum('bse,fe->bsf', x, W) + bias
            return y.reshape(b, seq_len, NUM_HEADS, HEAD_DIM).transpose(0, 2, 1, 3)
        q, k, v = (proj(Wq, bq), proj(Wk, bk), proj(Wv, bv))
        scores = jnp.einsum('bhqd,bhkd->bhqk', q, k) * SCALE
        mask = (adj_matrix + bond_matrix)[:, None, :, :]
        scores = scores * mask
        attn = jax.nn.softmax(scores, axis=-1)
        ctx = jnp.einsum('bhqk,bhkd->bhqd', attn, v)
        ctx = ctx.transpose(0, 2, 1, 3).reshape(b, seq_len, EMBED_DIM)
        return jnp.einsum('bse,fe->bsf', ctx, Wo) + bo

    def _L2_gnn_ref(x, adj, W):
        import jax, jax.numpy as jnp
        import numpy as np
        EPS = 1e-06
        deg = jnp.sum(adj, axis=-1, keepdims=True)
        agg = jnp.einsum('bij,bjf->bif', adj, x) / jnp.maximum(deg, EPS)
        cat = jnp.concatenate([x, agg], axis=2)
        out = jnp.einsum('bnf,of->bno', cat, W)
        return jax.nn.relu(out)

    def _L3_gnn_ref(X, A, Wv, bv, aw, ab, Wk, bk):
        import jax, jax.numpy as jnp
        import numpy as np
        B, N, DIN, DOUT, K = (4, 1024, 256, 256, 3)
        d = Wv.shape[1]
        Xw = X @ Wv + bv
        sj = Xw @ aw[:d, 0]
        si = Xw @ aw[d:, 0]
        e = jax.nn.leaky_relu(sj[:, None, :] + si[:, :, None] + ab[0], negative_slope=0.2)
        alpha_matrix = A * jnp.exp(e)
        transition = alpha_matrix / (jnp.sum(alpha_matrix, axis=-1, keepdims=True) + 1e-12)
        H = jnp.zeros(X.shape[:-1] + (d,), dtype=X.dtype)
        Xk = X
        for k in range(Wk.shape[0]):
            H = H + Xk @ Wk[k] + bk[k]
            Xk = jnp.einsum('bij,bjd->bid', transition, Xk)
        return jax.nn.relu(H)
    x = _layernorm(x + _L0_gnn_ref(x, adj, L0_gnn_W1, L0_gnn_b1, L0_gnn_gamma, L0_gnn_beta, L0_gnn_W2, L0_gnn_b2), axis=-1)
    x = _layernorm(x + _L1_gnn_ref(x, adj, adj, L1_gnn_Wq, L1_gnn_bq, L1_gnn_Wk, L1_gnn_bk, L1_gnn_Wv, L1_gnn_bv, L1_gnn_Wo, L1_gnn_bo, 512), axis=-1)
    x = _layernorm(x + _L2_gnn_ref(x, adj, L2_gnn_W), axis=-1)
    x = _layernorm(x + _L3_gnn_ref(x, adj, L3_gnn_Wv, L3_gnn_bv, L3_gnn_aw, L3_gnn_ab, L3_gnn_Wk, L3_gnn_bk), axis=-1)
    return x

_drawn_inputs = setup_inputs


def setup_inputs(seed=0):
    import zlib

    import numpy as np

    out = dict(_drawn_inputs(seed))
    spreads = {'L0_gnn_b1': (0.0, 0.1),
     'L0_gnn_gamma': (1.0, 0.2),
     'L0_gnn_beta': (0.0, 0.1),
     'L0_gnn_b2': (0.0, 0.1),
     'L1_gnn_bq': (0.0, 0.8),
     'L1_gnn_bk': (0.0, 0.8),
     'L1_gnn_bv': (0.0, 0.1),
     'L1_gnn_bo': (0.0, 0.1)}
    factors = {'L3_gnn_Wv': 3.358, 'L3_gnn_bv': 8.0, 'L3_gnn_aw': 4.507}
    for name, (base, spread) in spreads.items():
        noise = np.random.default_rng([zlib.crc32(name.encode()), seed]).standard_normal(out[name].shape)
        drawn = base * np.exp(spread * noise) if base else spread * noise
        out[name] = jnp.asarray(drawn.astype(out[name].dtype))
    for name, factor in factors.items():
        out[name] = (out[name] * factor).astype(out[name].dtype)
    return out
```

```python
from contextlib import ExitStack

import concourse.bass as bass
from concourse import mybir

F32 = mybir.dt.float32
F32R = mybir.dt.float32r
ACT = mybir.ActivationFunctionType
ALU = mybir.AluOpType

P = 128
HEADS = 8
HEAD_DIM = 32
GROUP = P // HEAD_DIM
TINY = 1.1754944e-38
LN_EPS = 1e-5
DEG_EPS = 1e-6
SUM_EPS = 1e-12
A_BANKS, B_BANKS = 5, 3
P_RING = 4
PT_RING = 8
EVAC_ON_VECTOR = (1, 4, 7)
STEPS = 39


class Batch:

    def __init__(self, reg, offset):
        self.reg, self.offset = reg, offset

    def at(self, per, n):
        if self.reg is None:
            return self.offset * per + n
        return self.reg * per + (self.offset * per + n)

    def index(self):
        return self.offset if self.reg is None else (self.reg if not self.offset else self.reg + self.offset)

    def first(self):
        return self.reg is None and self.offset == 0

    def before(self):
        return Batch(self.reg, self.offset - 1)


class Signal:

    def __init__(self, sem, per):
        self.sem, self.per = sem, per

    def at(self, batch, n):
        return batch.at(self.per, n)


class Chain:

    def __init__(self, sem, per):
        self.sem, self.per, self.n, self.batch = sem, per, 0, None

    def begin(self, batch):
        assert self.n in (0, self.per), (self.n, self.per)
        self.batch, self.n = batch, 0

    def link(self, eng, ins):
        self.n += 1
        ins.then_inc(self.sem, 1)
        eng.wait_ge(self.sem, self.batch.at(self.per, self.n))


class Ring:

    def __init__(self, banks, names, filled):
        self.banks, self.names, self.n, self.place = banks, names, len(banks), {x: i for i, x in enumerate(names)}
        self.filled, self.read = filled, {}
        self.uses = [len(range(k, len(names), self.n)) for k in range(self.n)]

    def bank(self, name):
        return self.banks[self.place[name] % self.n]

    def fill(self, name):
        return self.filled[self.place[name] % self.n]

    def full(self, batch, name):
        k, use = self.place[name] % self.n, self.place[name] // self.n
        return batch.at(self.uses[k], use + 1)

    def occupant(self, batch, name):
        i = self.place[name] - self.n
        if i >= 0:
            return self.names[i], batch
        if batch.first():
            return None, None
        k = self.place[name] % self.n
        return self.names[k + (self.uses[k] - 1) * self.n], batch.before()


def attention_parts(i, tiles):
    parts = []
    if i < tiles:
        parts.append(("s", i))
    if 3 <= i < tiles + 3:
        parts.append(("t", i - 3))
    if i >= 8 and (i - 8) % 4 == 0 and (i - 8) // 4 < tiles // 4:
        parts.append(("c", (i - 8) // 4))
    if i >= 14 and (i - 14) % 8 == 0 and (i - 14) // 8 < tiles // 8:
        parts.append(("o", (i - 14) // 8))
    return parts


def a_results(tiles):
    names = [f"ht{t}" for t in range(4)] + [f"m{t}" for t in range(4)] + ["dcol", "drow"]
    names += [f"g{t}" for t in range(2)] + [f"h{t}" for t in range(4)] + [f"z{t}" for t in range(4)]
    names += [f"n{t}" for t in range(4)] + [f"y{t}" for t in range(4)] + ["xt0", "xt1"]
    names += ["q0", "q1", "k0", "k1"] + [f"v{t}" for t in range(4)]
    for i in range(STEPS):
        names += [f"{kind}{n}" for kind, n in attention_parts(i, tiles)]
    return names


def b_results():
    names = [f"at{t}" for t in range(4)] + ["xt0", "xt1"] + [f"l{t}" for t in range(4)]
    names += [f"n{t}" for t in range(4)] + ["x3t0", "x3t1"]
    for t in range(4):
        names += [f"ya{t}", f"yb{t}"]
    return names + ["si"] + [f"u{t}" for t in range(4)] + [f"w{t}" for t in range(4)]


def round_schedule():
    order = [("B", "adj_t", t) for t in range(4)] + [("A", "load", 0)]
    order += [("B", "x2_t", 0)] + [("B", "linear", t) for t in range(4)]
    order += [("A", "incidence", 0), ("A", "split_x", 0)]
    order += [("B", "aggregate", t) for t in range(2)]
    order += [("A", "to_edges", t) for t in range(4)]
    order += [("B", "aggregate", t) for t in range(2, 4)]
    order += [("A", "degrees", 0), ("A", "to_nodes", 0)]
    order += [("B", "norm2", 0)]
    order += [("A", "hidden", t) for t in range(4)] + [("A", "project", 0)]
    order += [("B", "x3_t", 0)]
    order += [("A", "to_edges2", t) for t in range(4)] + [("A", "to_nodes2", 0), ("A", "x1_t", 0)]
    order += [("B", "mix", 0), ("B", "mix", 1)]
    order += [("A", "qk", 0), ("A", "values", 0)]
    order += [("B", "mix", 2), ("B", "mix", 3), ("B", "source", 0)]
    extra = {3: ("alpha", 0), 5: ("alpha", 1), 7: ("alpha", 2), 9: ("alpha", 3),
             13: ("hop1", 0), 15: ("hop1", 1), 17: ("hop1", 2), 19: ("hop1", 3),
             24: ("hop2", 0), 26: ("hop2", 1), 28: ("hop2", 2), 30: ("hop2", 3), 32: ("norm3", 0)}
    for i in range(STEPS):
        order.append(("A", "attend", i))
        if i in extra:
            order.append(("B", *extra[i]))
    return order


def build(nc, x, adj, W1, b1, gamma, beta, W2, b2, Wq, bq, Wk, bk, Wv, bv, Wo, bo, L2W,
          Pv, pbv, aw, ab, Wm, bm, out):
    BATCH, C, D = x.shape
    DH = W1.shape[0]
    K3 = Wm.shape[0]
    NT, DT, HT_ = C // P, D // P, DH // P
    TILES = NT * HEADS
    SCALE2 = 2.0 * HEAD_DIM ** -0.5
    MIX = K3 * D
    assert (C, D, DH, K3, HEADS * HEAD_DIM) == (512, 256, 512, 3, D)

    ctx = ExitStack()
    with ctx:
        cursor = [(nc.sbuf_base + 31) // 32 * 32]

        def place(name, shape, dt, at=None):
            size = 4
            for s in shape[1:]:
                size *= s
            size = (size + 31) // 32 * 32
            if at is None:
                at = cursor[0]
                cursor[0] += size
            assert at + size <= nc.sbuf_usable_end, (name, at + size)
            return nc.alloc_sbuf_tensor_at(name, shape, dt, offset=at)

        def sem(name):
            return ctx.enter_context(nc.semaphore(name))

        def signal(name, per):
            return Signal(sem(name), per)

        w1t_hi, w1t_lo = (place(f"w1t_{s}", [P, DT, DH], F32R) for s in ("hi", "lo"))
        w2c_hi = place("w2c_hi", [P, HT_, D + 2], F32R)
        w2c_lo = place("w2c_lo", [P, HT_, D], F32R)
        wqt_hi, wqt_lo = (place(f"wqt_{s}", [P, DT, D], F32R) for s in ("hi", "lo"))
        wkt_hi, wkt_lo = (place(f"wkt_{s}", [P, DT, D], F32R) for s in ("hi", "lo"))
        wvt_hi, wvt_lo = (place(f"wvt_{s}", [P, DT, D], F32R) for s in ("hi", "lo"))
        wot_hi, wot_lo = (place(f"wot_{s}", [P, DT, D], F32R) for s in ("hi", "lo"))
        l2t_hi, l2t_lo = (place(f"l2t_{s}", [P, DT, 2 * D], F32R) for s in ("hi", "lo"))
        mix_hi, mix_lo = (place(f"mix_{s}", [P, DT, MIX + 2], F32R) for s in ("hi", "lo"))
        urep_hi, urep_lo = (place(f"urep_{s}", [P, DT, P], F32R) for s in ("hi", "lo"))
        b2_row = place("b2_row", [P, D], F32)
        betaw2_row = place("betaw2_row", [P, D], F32)
        bv_row = place("bv_row", [P, D], F32)
        bo_row = place("bo_row", [P, D], F32)
        bm_row = place("bm_row", [P, D], F32)
        ident = place("ident", [P, P], F32)
        ones = place("ones", [P, 8], F32)
        half_neg = place("half_neg", [P, 4], F32)
        cols = place("cols", [P, 24], F32)
        b1_col, gamma_col, beta_col = cols[:, 0:4], cols[:, 4:8], cols[:, 8:12]
        bq_col, bk_col, shift_col = cols[:, 12:14], cols[:, 14:16], cols[:, 16:17]

        weights_end = cursor[0]

        at = cursor[0]
        cursor[0] += 16384
        inc = place("inc", [P, NT, C], F32R, at)
        inc_t = place("inc_t", [P, NT, C], F32R, at + 8192)
        q_pack = place("q_pack", [P, HEADS, C], F32R, at)
        at = cursor[0]
        cursor[0] += 16384
        h_hi = place("h_hi", [P, HT_, C], F32R, at)
        h_lo = place("h_lo", [P, HT_, C], F32R, at + 8192)
        k_pack = place("k_pack", [P, HEADS, C], F32R, at)
        at = cursor[0]
        cursor[0] += 16384
        m_hi = place("m_hi", [P, NT, D], F32R, at)
        m_lo = place("m_lo", [P, NT, D], F32R, at + 4096)
        g_hi = place("g_hi", [P, DT, C], F32R, at + 8192)
        g_lo = place("g_lo", [P, DT, C], F32R, at + 12288)
        q_hi = place("q_hi", [P, DT, C], F32R, at)
        q_lo = place("q_lo", [P, DT, C], F32R, at + 4096)
        k_hi = place("k_hi", [P, DT, C], F32R, at + 8192)
        k_lo = place("k_lo", [P, DT, C], F32R, at + 12288)
        probs_t = place("probs_t", [P, PT_RING, NT, P], F32, at)
        at = cursor[0]
        cursor[0] += 8224
        x_hi = place("x_hi", [P, NT, D + 2], F32R, at)
        x_lo = place("x_lo", [P, NT, D], F32R, at + 4128)
        z_hi = place("z_hi", [P, NT, D], F32R, at)
        z_lo = place("z_lo", [P, NT, D], F32R, at + 4128)
        x1t_hi = place("x1t_hi", [P, DT, C], F32R, at)
        x1t_lo = place("x1t_lo", [P, DT, C], F32R, at + 4128)
        mask = place("mask", [P, NT, C], F32)
        x_in = place("x_in", [P, NT, D], F32)
        x1 = place("x1", [P, NT, D], F32)
        values = place("values", [P, NT, D], F32)
        at = cursor[0]
        cursor[0] += 8192
        probs = place("probs", [P, P_RING, C], F32, at)
        squares = place("squares", [P, HT_, C], F32, at)
        w_rep_hi = place("w_rep_hi", [P, NT, P], F32R, at)
        w_rep_lo = place("w_rep_lo", [P, NT, P], F32R, at + 2048)
        dn_row = place("dn_row", [P, C], F32, at + 4096)
        tmp_a = place("tmp_a", [P, 2, C], F32)
        recip_rep = place("recip_rep", [P, 2, P], F32)
        recip_t = place("recip_t", [P, 2, P], F32)
        cx_hi = place("cx_hi", [P, DT, P], F32R)
        cx_lo = place("cx_lo", [P, DT, P], F32R)
        w_col = place("w_col", [P, NT], F32)
        w_hl = place("w_hl", [P, NT, 2], F32R)
        be = place("be", [P, NT], F32)
        be_t = place("be_t", [P, NT], F32)
        dn = place("dn", [P, NT], F32)
        dn_t = place("dn_t", [P, 2, NT], F32)
        stat = place("stat", [P, 5, NT], F32)
        bn_a = place("bn_a", [P, NT, 6], F32)
        mv_a = place("mv_a", [P, NT, 2], F32)
        ve_a = place("ve_a", [P, NT], F32)
        rs_a = place("rs_a", [P, NT], F32)
        top = place("top", [P, TILES], F32)
        neg_top = place("neg_top", [P, TILES], F32)
        sums = place("sums", [P, TILES], F32)
        rsum = place("rsum", [P, TILES], F32)

        adjt_hi, adjt_lo = (place(f"adjt_{s}", [P, NT, C], F32R) for s in ("hi", "lo"))
        x2 = place("x2", [P, NT, D], F32)
        x3 = place("x3", [P, NT, D], F32)
        at = cursor[0]
        cursor[0] += 8192
        xt_hi = place("xt_hi", [P, DT, C], F32R, at)
        xt_lo = place("xt_lo", [P, DT, C], F32R, at + 4096)
        v_hi = place("v_hi", [P, NT, D], F32R, at)
        v_lo = place("v_lo", [P, NT, D], F32R, at + 4096)
        y01 = place("y01", [P, NT, 2 * D], F32)
        y_hi = place("y_hi", [P, NT, D + 2], F32R)
        y_lo = place("y_lo", [P, NT, D], F32R)
        si_row = place("si_row", [P, C], F32)
        e_tmp = place("e_tmp", [P, C], F32)
        at = cursor[0]
        al_tmp = place("al_tmp", [P, C], F32)
        v_tmp = place("v_tmp", [P, D], F32, at)
        sj_col = place("sj_col", [P, NT], F32)
        bdeg = place("bdeg", [P, 2, NT], F32)
        bn_b = place("bn_b", [P, NT, 6], F32)
        mv_b = place("mv_b", [P, NT, 2], F32)
        ve_b = place("ve_b", [P, NT], F32)
        rs_b = place("rs_b", [P, NT], F32)

        banks = [ctx.enter_context(nc.psum_tensor(f"bank{k}", [P, 512], F32)) for k in range(8)]
        ring_a = Ring(banks[:A_BANKS], a_results(TILES), [sem(f"a_filled{k}") for k in range(A_BANKS)])
        ring_b = Ring(banks[A_BANKS:], b_results(), [sem(f"b_filled{k}") for k in range(B_BANKS)])

        def plain(ap):
            return ap.bitcast(F32)

        prepare(nc, ctx, locals())
        rounds(nc, ctx, locals())


def prepare(nc, ctx, v):
    g = dict(v)
    (place, sem, banks, ident, ones, cols, plain) = (g[k] for k in ("place", "sem", "banks", "ident", "ones", "cols", "plain"))
    DT, HT_, D, DH, MIX, K3, C = (g[k] for k in ("DT", "HT_", "D", "DH", "MIX", "K3", "C"))
    spot = [g["weights_end"]]

    def staged(name, shape, dt=F32):
        size = 4
        for s in shape[1:]:
            size *= s
        at = spot[0]
        spot[0] += (size + 31) // 32 * 32
        return nc.alloc_sbuf_tensor_at(name, shape, dt, offset=at)

    w1n = staged("w1n", [P, HT_, D])
    w2n = staged("w2n", [P, DT, DH])
    wn = {n: staged(f"{n}_n", [P, DT, D]) for n in ("q", "k", "v", "o")}
    l2n = staged("l2n", [P, DT, 2 * D])
    w2t = staged("w2t", [P, HT_, D])
    mixn = staged("mixn", [P, DT, MIX + 2])
    pvn = staged("pvn", [P, DT, D])
    aw_row = staged("aw_row", [P, 2 * D])
    pbv_row = staged("pbv_row", [P, D])
    bm_rows = staged("bm_rows", [P, K3 * D])
    gamma_rep = staged("gamma_rep", [P, HT_, P])
    beta_rep = staged("beta_rep", [P, HT_, P])
    u_rep = staged("u_rep", [P, DT, P])
    w2s = staged("w2s", [P, HT_, D])
    junk = staged("junk", [P, 6, D])
    dots = staged("dots", [P, 8])
    loaded = sem("weights_loaded")
    const = sem("constants_ready")
    turned = sem("weights_turned")
    high = sem("weights_high")
    low = sem("weights_low")
    reps = sem("weights_rep")
    chain = sem("weights_chain")
    rows = sem("weights_rows")

    items = []
    for t in range(DT):
        items.append(([w1n[:, s, t * P:(t + 1) * P] for s in range(HT_)], g["w1t_hi"][:, t, :], g["w1t_lo"][:, t, :]))
    for n in ("q", "k", "v", "o"):
        for t in range(DT):
            items.append(([wn[n][:, s, t * P:(t + 1) * P] for s in range(DT)],
                          g[f"w{n}t_hi"][:, t, :], g[f"w{n}t_lo"][:, t, :]))
    for t in range(DT):
        items.append(([l2n[:, s, half * D + t * P:half * D + (t + 1) * P] for half in range(2) for s in range(DT)],
                      g["l2t_hi"][:, t, :], g["l2t_lo"][:, t, :]))
    n_split = len(items)
    for t in range(HT_):
        items.append(([w2n[:, s, t * P:(t + 1) * P] for s in range(DT)], w2t[:, t, :], None))

    def col(vec, n):
        return vec.rearrange("(t p) -> p t", p=P)

    loads = [
        (w1n[:], g["W1"].rearrange("(t p) d -> p t d", p=P)),
        (wn["q"][:], g["Wq"].rearrange("(t p) d -> p t d", p=P)),
        (wn["k"][:], g["Wk"].rearrange("(t p) d -> p t d", p=P)),
        (wn["v"][:], g["Wv"].rearrange("(t p) d -> p t d", p=P)),
        (wn["o"][:], g["Wo"].rearrange("(t p) d -> p t d", p=P)),
        (l2n[:], g["L2W"].rearrange("(t p) d -> p t d", p=P)),
        (w2n[:], g["W2"].rearrange("(t p) d -> p t d", p=P)),
        (pvn[:], g["Pv"].rearrange("(t p) d -> p t d", p=P)),
        (aw_row[:], g["aw"].rearrange("a b -> (a b)").partition_broadcast(P)),
        (pbv_row[:], g["pbv"].partition_broadcast(P)),
        (bm_rows[:], g["bm"].rearrange("k d -> (k d)").partition_broadcast(P)),
        (g["b2_row"][:], g["b2"].partition_broadcast(P)),
        (g["bv_row"][:], g["bv"].partition_broadcast(P)),
        (g["bo_row"][:], g["bo"].partition_broadcast(P)),
        (cols[:, 17:18], g["ab"].partition_broadcast(P)),
    ] + [(mixn[:, :, k * D:(k + 1) * D], g["Wm"][k].rearrange("(t p) d -> p t d", p=P)) for k in range(K3)]
    small = [(g["b1_col"], g["b1"]), (g["gamma_col"], g["gamma"]), (g["beta_col"], g["beta"]),
             (g["bq_col"], g["bq"]), (g["bk_col"], g["bk"])]

    with nc.Block() as block:
        @block.sync
        def _(sp):
            for dst, src in loads:
                sp.dma_start(dst, src).then_inc(loaded, 16)
            with nc.allow_non_contiguous_dma(reason="bias vectors, once"):
                for dst, src in small:
                    sp.dma_start(dst, col(src, 0)).then_inc(loaded, 16)
            sp.wait_ge(loaded, 16 * (len(loads) + len(small)))

        @block.gpsimd
        def _(pool):
            pool.memset(ident[:], 0.0).then_inc(const, 1)
            pool.memset(ones[:], 1.0).then_inc(const, 1)
            pool.memset(g["half_neg"][:], -0.5).then_inc(const, 1)
            pool.wait_ge(const, 3)
            pool.affine_select(out=ident[:], in_=ident[:], compare_op=ALU.not_equal, fill=1.0, base=0,
                               pattern=[[-1, P]], channel_multiplier=1).then_inc(const, 1)

        @block.tensor
        def _(pe):
            pe.wait_ge(const, 4)
            pe.wait_ge(loaded, 16 * (len(loads) + len(small)))
            for n, (srcs, hi, lo) in enumerate(items):
                if n >= 8:
                    pe.wait_ge(low, n - 7)
                for s, src in enumerate(srcs):
                    last = pe.transpose(banks[n % 8][:, s * P:(s + 1) * P], src, ident[:])
                last.then_inc(turned, 1)
            pe.wait_ge(low, len(items))
            pe.wait_ge(reps, 1)
            for n, rep in enumerate((gamma_rep, beta_rep)):
                for t in range(HT_):
                    last = pe.matmul(banks[n][:, 0:D], rep[:, t, :], w2t[:, t, :], start=t == 0, stop=t == HT_ - 1)
                last.then_inc(turned, 1)

        @block.scalar
        def _(act):
            for n, (srcs, hi, lo) in enumerate(items):
                act.wait_ge(turned, n + 1)
                act.activation(hi, banks[n % 8][:, 0:len(srcs) * P], ACT.Copy).then_inc(high, 1)
            act.wait_ge(turned, len(items) + 2)
            act.activation(g["betaw2_row"][:], banks[1][:, 0:D], ACT.Copy).then_inc(rows, 1)
            act.wait_ge(const, 4)
            for t in range(HT_):
                act.activation(g["w2c_hi"][:, t, D:D + 2], ones[:, 0:2], ACT.Copy).then_inc(rows, 1)
                act.activation(g["y_hi"][:, t, D:D + 2], ones[:, 0:2], ACT.Copy).then_inc(rows, 1)

        @block.vector
        def _(dve):
            count = [0]

            def link(ins):
                count[0] += 1
                ins.then_inc(chain, 1)
                dve.wait_ge(chain, count[0])

            dve.wait_ge(loaded, 16 * (len(loads) + len(small)))
            dve.wait_ge(const, 4)
            for t in range(HT_):
                dve.tensor_scalar(gamma_rep[:, t, :], ones[:, 0:1].to_broadcast([P, P]), g["gamma_col"][:, t:t + 1],
                                  1.0 / DH, ALU.mult, ALU.mult)
                last = dve.tensor_scalar(beta_rep[:, t, :], ones[:, 0:1].to_broadcast([P, P]),
                                         g["beta_col"][:, t:t + 1], None, ALU.mult)
            last.then_inc(reps, 1)
            for n, (srcs, hi, lo) in enumerate(items):
                dve.wait_ge(high, n + 1)
                if lo is None:
                    dve.tensor_copy(dots[:, 4:5], ones[:, 0:1]).then_inc(low, 1)
                    dve.wait_ge(low, n + 1)
                else:
                    dve.tensor_tensor(lo, banks[n % 8][:, 0:len(srcs) * P], plain(hi), ALU.subtract).then_inc(low, 1)
            dve.wait_ge(turned, len(items) + 1)
            for t in range(HT_):
                link(dve.scalar_tensor_tensor(out=w2s[:, t, :], in0=w2t[:, t, :], scalar=g["gamma_col"][:, t:t + 1],
                                              in1=banks[0][:, 0:D], op0=ALU.mult, op1=ALU.subtract))
                link(dve.tensor_copy(g["w2c_hi"][:, t, 0:D], w2s[:, t, :]))
                link(dve.tensor_tensor(g["w2c_lo"][:, t, :], w2s[:, t, :], plain(g["w2c_hi"][:, t, 0:D]), ALU.subtract))
            for t in range(DT):
                for s in range(2):
                    link(dve.tensor_tensor_reduce(junk[:, 2 * t + s, :], pvn[:, t, :], aw_row[:, s * D:(s + 1) * D], 1.0, 0.0,
                                                  ALU.mult, ALU.add, dots[:, 2 * t + s:2 * t + s + 1]))
                link(dve.tensor_copy(mixn[:, t, MIX:MIX + 2], dots[:, 2 * t:2 * t + 1].to_broadcast([P, 2])))
                link(dve.tensor_scalar(u_rep[:, t, :], ones[:, 0:1].to_broadcast([P, P]),
                                       dots[:, 2 * t + 1:2 * t + 2], None, ALU.mult))
            for s in range(2):
                link(dve.tensor_tensor_reduce(junk[:, 4 + s, :], pbv_row[:], aw_row[:, s * D:(s + 1) * D], 1.0, 0.0,
                                              ALU.mult, ALU.add, dots[:, 6 + s:7 + s]))
            link(dve.tensor_tensor(dots[:, 5:6], dots[:, 6:7], dots[:, 7:8], ALU.add))
            link(dve.tensor_tensor(g["shift_col"], dots[:, 5:6], cols[:, 17:18], ALU.add))
            link(dve.tensor_copy(g["mix_hi"][:], mixn[:]))
            link(dve.tensor_tensor(g["mix_lo"][:], mixn[:], plain(g["mix_hi"][:]), ALU.subtract))
            link(dve.tensor_copy(g["urep_hi"][:], u_rep[:]))
            link(dve.tensor_tensor(g["urep_lo"][:], u_rep[:], plain(g["urep_hi"][:]), ALU.subtract))
            link(dve.tensor_tensor(g["bm_row"][:], bm_rows[:, 0:D], bm_rows[:, D:2 * D], ALU.add))
            link(dve.tensor_tensor(g["bm_row"][:], g["bm_row"][:], bm_rows[:, 2 * D:3 * D], ALU.add))


def rounds(nc, ctx, v):
    names = ("signal sem ring_a ring_b plain ident ones half_neg b1_col bq_col bk_col shift_col b2_row betaw2_row "
             "bv_row bo_row bm_row w1t_hi w1t_lo w2c_hi w2c_lo wqt_hi wqt_lo wkt_hi wkt_lo wvt_hi wvt_lo wot_hi "
             "wot_lo l2t_hi l2t_lo mix_hi mix_lo urep_hi urep_lo inc inc_t q_pack k_pack h_hi h_lo m_hi m_lo g_hi "
             "g_lo q_hi q_lo k_hi k_lo probs_t x_hi x_lo z_hi z_lo x1t_hi x1t_lo mask x_in x1 values probs squares "
             "w_rep_hi w_rep_lo dn_row tmp_a recip_rep recip_t cx_hi cx_lo w_col w_hl be be_t dn dn_t stat bn_a "
             "mv_a ve_a rs_a top neg_top sums rsum adjt_hi adjt_lo x2 x3 xt_hi xt_lo v_hi v_lo y01 y_hi y_lo "
             "si_row e_tmp al_tmp v_tmp sj_col bdeg bn_b mv_b ve_b rs_b x adj out BATCH C D DH NT DT HT_ TILES "
             "SCALE2 MIX")
    (signal, sem, ring_a, ring_b, plain, ident, ones, half_neg, b1_col, bq_col, bk_col, shift_col, b2_row, betaw2_row,
     bv_row, bo_row, bm_row, w1t_hi, w1t_lo, w2c_hi, w2c_lo, wqt_hi, wqt_lo, wkt_hi, wkt_lo, wvt_hi, wvt_lo, wot_hi,
     wot_lo, l2t_hi, l2t_lo, mix_hi, mix_lo, urep_hi, urep_lo, inc, inc_t, q_pack, k_pack, h_hi, h_lo, m_hi, m_lo,
     g_hi, g_lo, q_hi, q_lo, k_hi, k_lo, probs_t, x_hi, x_lo, z_hi, z_lo, x1t_hi, x1t_lo, mask, x_in, x1, values,
     probs, squares, w_rep_hi, w_rep_lo, dn_row, tmp_a, recip_rep, recip_t, cx_hi, cx_lo, w_col, w_hl, be, be_t, dn,
     dn_t, stat, bn_a, mv_a, ve_a, rs_a, top, neg_top, sums, rsum, adjt_hi, adjt_lo, x2, x3, xt_hi, xt_lo, v_hi,
     v_lo, y01, y_hi, y_lo, si_row, e_tmp, al_tmp, v_tmp, sj_col, bdeg, bn_b, mv_b, ve_b, rs_b, x, adj, out, BATCH,
     C, D, DH, NT, DT, HT_, TILES, SCALE2, MIX) = (v[k] for k in names.split())

    settled = {e: sem(f"settled_{e}") for e in ("sp", "pool", "vector")}
    adj_in, x_loaded = signal("adj_in", 16), signal("x_loaded", 16)
    inc_ready, inc_t_ready = signal("inc_ready", 4), signal("inc_t_ready", 4)
    w_ready = signal("w_ready", 1)
    x_hi_ready, x_lo_ready, x2b_ready = signal("x_hi_ready", 1), signal("x_lo_ready", 1), signal("x2b_ready", 1)
    be_ready = signal("be_ready", 4)
    m_hi_ready, m_lo_ready = signal("m_hi_ready", 8), signal("m_lo_ready", 8)
    g_ready, g_hi_ready, g_lo_ready = signal("g_ready", 2), signal("g_hi_ready", 2), signal("g_lo_ready", 2)
    h_ready, h_hi_ready, h_lo_ready = signal("h_ready", 4), signal("h_hi_ready", 4), signal("h_lo_ready", 4)
    sq_ready = signal("sq_ready", 4)
    var_ready, rstd_ready = signal("var_ready", 6), signal("rstd_ready", 6)
    z_ready, z_hi_ready, z_lo_ready = signal("z_ready", 4), signal("z_hi_ready", 4), signal("z_lo_ready", 4)
    x1_ready, x1b_ready = signal("x1_ready", 4), signal("x1b_ready", 1)
    x1t_hi_ready, x1t_lo_ready = signal("x1t_hi_ready", 2), signal("x1t_lo_ready", 2)
    qk_hi_ready, qk_lo_ready = signal("qk_hi_ready", 4), signal("qk_lo_ready", 4)
    values_ready = signal("values_ready", 4)
    packed = signal("packed", 16 * 2 * GROUP * GROUP)
    masked, top_ready = signal("masked", TILES), signal("top_ready", TILES)
    probs_ready = signal("probs_ready", TILES)
    on_vector = [i for i in range(TILES) if i % HEADS in EVAC_ON_VECTOR]
    on_scalar = [i for i in range(TILES) if i % HEADS not in EVAC_ON_VECTOR]
    pt_vector, pt_scalar = signal("pt_vector", len(on_vector)), signal("pt_scalar", len(on_scalar))
    rrep_ready, rt_ready = signal("rrep_ready", 8), signal("rt_ready", 8)
    cx_ready, cx_hi_ready, cx_lo_ready = signal("cx_ready", 8), signal("cx_hi_ready", 8), signal("cx_lo_ready", 8)
    x2_ready = signal("x2_ready", 4)
    adjt_hi_ready, adjt_lo_ready = signal("adjt_hi_ready", 8), signal("adjt_lo_ready", 8)
    xt_hi_ready, xt_lo_ready = signal("xt_hi_ready", 4), signal("xt_lo_ready", 4)
    y_hi_ready, y_lo_ready, y01_ready = signal("y_hi_ready", 8), signal("y_lo_ready", 8), signal("y01_ready", 8)
    var_b, rstd_b = signal("var_b", 2), signal("rstd_b", 2)
    x3_ready = signal("x3_ready", 4)
    sj_ready, si_ready, lrelu_ready, exp_ready = (signal("sj_ready", 4), signal("si_ready", 1),
                                                  signal("lrelu_ready", 4), signal("exp_ready", 4))
    alpha_ready = signal("alpha_ready", 4)
    dcol_read, drow_ready = signal("dcol_read", 1), signal("drow_ready", 1)
    y_read, o_read, n_read, w_read = (signal(f"{k}_read", 4) for k in "yonw")
    y0_ready = signal("y0_ready", 4)
    v_ready, v_hi_ready, v_lo_ready = signal("v_ready", 4), signal("v_hi_ready", 4), signal("v_lo_ready", 4)
    out_ready, stored = signal("out_ready", 1), signal("stored", 16)
    chain_a, chain_b = Chain(sem("vector_chain_a"), 46), Chain(sem("vector_chain_b"), 44)
    pool_a, pool_b = Chain(sem("pool_chain_a"), 1), Chain(sem("pool_chain_b"), 4)
    act_a = Chain(sem("scalar_chain_a"), 1)
    chains = {"dve": (chain_a, chain_b), "pool": (pool_a, pool_b), "act": (act_a, None)}

    def settle(eng, who):
        eng.sem_inc(settled[who], 1)

    def pt_done(eng, a, i):
        if i in on_vector:
            eng.wait_ge(pt_vector.sem, pt_vector.at(a, on_vector.index(i) + 1))
        else:
            eng.wait_ge(pt_scalar.sem, pt_scalar.at(a, on_scalar.index(i) + 1))

    def both_pt_done(eng, a, i):
        nv, ns = sum(j <= i for j in on_vector), sum(j <= i for j in on_scalar)
        if nv:
            eng.wait_ge(pt_vector.sem, pt_vector.at(a, nv))
        if ns:
            eng.wait_ge(pt_scalar.sem, pt_scalar.at(a, ns))

    for t in range(4):
        ring_a.read.update({f"ht{t}": (inc_t_ready, t + 1), f"m{t}": (m_lo_ready, t + 1), f"h{t}": (h_ready, t + 1),
                            f"z{t}": (z_ready, t + 1), f"n{t}": (m_lo_ready, NT + t + 1), f"y{t}": (y_read, t + 1),
                            f"v{t}": (values_ready, t + 1), f"o{t}": (o_read, t + 1)})
        ring_b.read.update({f"at{t}": (adjt_lo_ready, t + 1), f"l{t}": (y_lo_ready, t + 1), f"n{t}": (n_read, t + 1),
                            f"ya{t}": (y0_ready, t + 1), f"yb{t}": (y_lo_ready, NT + t + 1),
                            f"u{t}": (v_ready, t + 1), f"w{t}": (w_read, t + 1)})
    for t in range(2):
        ring_a.read.update({f"g{t}": (g_ready, t + 1), f"xt{t}": (x1t_lo_ready, t + 1), f"q{t}": (qk_lo_ready, t + 1),
                            f"k{t}": (qk_lo_ready, DT + t + 1)})
        ring_b.read.update({f"xt{t}": (xt_lo_ready, t + 1), f"x3t{t}": (xt_lo_ready, DT + t + 1)})
    ring_a.read.update(dcol=(dcol_read, 1), drow=(drow_ready, 1))
    ring_b.read.update(si=(si_ready, 1))
    for i in range(TILES):
        ring_a.read[f"s{i}"] = (masked, i + 1)
        ring_a.read[f"t{i}"] = (pt_vector, on_vector.index(i) + 1) if i in on_vector else \
                               (pt_scalar, on_scalar.index(i) + 1)
    for n in range(TILES // GROUP):
        ring_a.read[f"c{n}"] = (cx_ready, n + 1)

    order = round_schedule()

    def drive(eng, stages, links=(None, None)):
        def one(a, b):
            for c, batch in zip(links, (a, b)):
                if c is not None and batch is not None:
                    c.begin(batch)
            for thread, name, n in order:
                batch = a if thread == "A" else b
                if batch is not None and (thread, name) in stages:
                    stages[thread, name](batch, n)

        one(Batch(None, 0), None)
        one(Batch(None, 1), Batch(None, 0))
        with eng.Fori(2, BATCH) as r:
            one(Batch(r, 0), Batch(r, -1))
        one(None, Batch(None, BATCH - 1))

    with nc.Block() as block:
        @block.sync
        def _(sp):
            def load(a, _):
                if not a.first():
                    sp.wait_ge(adjt_hi_ready.sem, adjt_hi_ready.at(a.before(), 4))
                    settle(sp, "sp")
                sp.dma_start(mask[:], adj[a.index()].rearrange("(t p) c -> p t c", p=P)).then_inc(adj_in.sem, 16)
                if not a.first():
                    sp.wait_ge(x1_ready.sem, x1_ready.at(a.before(), 4))
                    settle(sp, "sp")
                sp.dma_start(x_in[:], x[a.index()].rearrange("(t p) d -> p t d", p=P)).then_inc(x_loaded.sem, 16)

            def qk(a, _):
                for n, (hi, lo, pack, blocks) in enumerate(((q_hi, q_lo, q_pack, (0, 0, 1, 1)),
                                                            (k_hi, k_lo, k_pack, (0, 1, 0, 1)))):
                    sp.wait_ge(qk_hi_ready.sem, qk_hi_ready.at(a, 2 * n + 2))
                    sp.wait_ge(qk_lo_ready.sem, qk_lo_ready.at(a, 2 * n + 2))
                    settle(sp, "sp")
                    for h in range(GROUP):
                        rows = slice(h * HEAD_DIM, (h + 1) * HEAD_DIM)
                        for block_row, part in enumerate(blocks):
                            to = slice(block_row * HEAD_DIM, (block_row + 1) * HEAD_DIM)
                            sp.dma_start(plain(pack[to, h:HEADS:GROUP, :]), plain((hi, lo)[part][rows, :, :]))\
                              .then_inc(packed.sem, 16)

            def norm3(b, _):
                sp.wait_ge(out_ready.sem, out_ready.at(b, 1))
                settle(sp, "sp")
                sp.dma_start(out[b.index()].rearrange("(t p) d -> p t d", p=P), y01[:, :, 0:D]).then_inc(stored.sem, 16)

            drive(sp, {("A", "load"): load, ("A", "qk"): qk, ("B", "norm3"): norm3})
            sp.wait_ge(stored.sem, 16 * BATCH + 16)

        @block.tensor
        def _(pe):
            def take(ring, batch, name):
                before, its_batch = ring.occupant(batch, name)
                if before is not None:
                    signal_of, n = ring.read[before]
                    pe.wait_ge(signal_of.sem, signal_of.at(its_batch, n))
                return ring.bank(name)

            def split_products(bank, parts, wide, width):
                for n, (l_hi, l_lo, r_hi, r_lo) in enumerate(parts):
                    pe.matmul(bank[:, 0:wide], l_hi, r_hi, start=n == 0, stop=False)
                    pe.matmul(bank[:, 0:wide], l_lo, r_hi, start=False, stop=False)
                    last = pe.matmul(bank[:, 0:width], l_hi, r_lo, start=False, stop=n == len(parts) - 1)
                return last

            def c(t):
                return slice(t * P, (t + 1) * P)

            def incidence(a, _):
                pe.wait_ge(adj_in.sem, adj_in.at(a, 16))
                for t in range(NT):
                    bank = take(ring_a, a, f"ht{t}")
                    for s in range(NT):
                        last = pe.transpose(bank[:, c(s)], mask[:, s, c(t)], ident[:])
                    last.then_inc(ring_a.fill(f"ht{t}"), 1)

            def to_edges(a, t):
                if t == 0:
                    pe.wait_ge(inc_ready.sem, inc_ready.at(a, NT))
                    pe.wait_ge(x_hi_ready.sem, x_hi_ready.at(a, 1))
                    pe.wait_ge(x_lo_ready.sem, x_lo_ready.at(a, 1))
                bank = take(ring_a, a, f"m{t}")
                for s in range(NT):
                    pe.matmul(bank[:, 0:D + 2], inc[:, s, c(t)], x_hi[:, s, :], start=s == 0, stop=False)
                    last = pe.matmul(bank[:, 0:D], inc[:, s, c(t)], x_lo[:, s, :], start=False, stop=s == NT - 1)
                last.then_inc(ring_a.fill(f"m{t}"), 1)

            def degrees(a, _):
                pe.wait_ge(w_ready.sem, w_ready.at(a, 1))
                bank = take(ring_a, a, "dcol")
                for t in range(NT):
                    for s in range(NT):
                        last = pe.matmul(bank[:, 2 * t:2 * t + 2], inc_t[:, s, c(t)], w_hl[:, s, :],
                                         start=s == 0, stop=s == NT - 1)
                last.then_inc(ring_a.fill("dcol"), 1)
                bank = take(ring_a, a, "drow")
                for s in range(NT):
                    pe.matmul(bank[:], w_rep_hi[:, s, :], inc_t[:, s, :], start=s == 0, stop=False)
                    last = pe.matmul(bank[:], w_rep_lo[:, s, :], inc_t[:, s, :], start=False, stop=s == NT - 1)
                last.then_inc(ring_a.fill("drow"), 1)

            def to_nodes(a, _):
                pe.wait_ge(m_hi_ready.sem, m_hi_ready.at(a, 4))
                pe.wait_ge(m_lo_ready.sem, m_lo_ready.at(a, 4))
                for t in range(DT):
                    bank = take(ring_a, a, f"g{t}")
                    for s in range(NT):
                        pe.matmul(bank[:], m_hi[:, s, c(t)], inc_t[:, s, :], start=s == 0, stop=False)
                        last = pe.matmul(bank[:], m_lo[:, s, c(t)], inc_t[:, s, :], start=False, stop=s == NT - 1)
                    last.then_inc(ring_a.fill(f"g{t}"), 1)

            def hidden(a, t):
                if t == 0:
                    pe.wait_ge(g_hi_ready.sem, g_hi_ready.at(a, 2))
                    pe.wait_ge(g_lo_ready.sem, g_lo_ready.at(a, 2))
                bank = take(ring_a, a, f"h{t}")
                last = split_products(bank, [(w1t_hi[:, s, c(t)], w1t_lo[:, s, c(t)], g_hi[:, s, :], g_lo[:, s, :])
                                             for s in range(DT)], C, C)
                last.then_inc(ring_a.fill(f"h{t}"), 1)

            def project(a, _):
                pe.wait_ge(h_hi_ready.sem, h_hi_ready.at(a, 4))
                pe.wait_ge(h_lo_ready.sem, h_lo_ready.at(a, 4))
                pe.wait_ge(sq_ready.sem, sq_ready.at(a, 4))
                for t in range(NT):
                    bank = take(ring_a, a, f"z{t}")
                    split_products(bank, [(h_hi[:, s, c(t)], h_lo[:, s, c(t)], w2c_hi[:, s, :], w2c_lo[:, s, :])
                                          for s in range(HT_)], D + 2, D)
                    for s in range(HT_):
                        last = pe.matmul(bank[:, D + 4:D + 5], squares[:, s, c(t)], ones[:, 0:1],
                                         start=False, stop=s == HT_ - 1, skip_group_check=True)
                    last.then_inc(ring_a.fill(f"z{t}"), 1)

            def to_edges2(a, t):
                if t == 0:
                    pe.wait_ge(z_hi_ready.sem, z_hi_ready.at(a, 4))
                    pe.wait_ge(z_lo_ready.sem, z_lo_ready.at(a, 4))
                bank = take(ring_a, a, f"n{t}")
                for s in range(NT):
                    pe.matmul(bank[:, 0:D], inc[:, s, c(t)], z_hi[:, s, :], start=s == 0, stop=False)
                    last = pe.matmul(bank[:, 0:D], inc[:, s, c(t)], z_lo[:, s, :], start=False, stop=s == NT - 1)
                last.then_inc(ring_a.fill(f"n{t}"), 1)

            def to_nodes2(a, _):
                pe.wait_ge(m_hi_ready.sem, m_hi_ready.at(a, 8))
                pe.wait_ge(m_lo_ready.sem, m_lo_ready.at(a, 8))
                for t in range(NT):
                    bank = take(ring_a, a, f"y{t}")
                    for s in range(NT):
                        pe.matmul(bank[:, 0:D], inc_t[:, s, c(t)], m_hi[:, s, :], start=s == 0, stop=False)
                        last = pe.matmul(bank[:, 0:D], inc_t[:, s, c(t)], m_lo[:, s, :], start=False, stop=s == NT - 1)
                    last.then_inc(ring_a.fill(f"y{t}"), 1)

            def x1_t(a, _):
                pe.wait_ge(x1_ready.sem, x1_ready.at(a, 4))
                for t in range(DT):
                    bank = take(ring_a, a, f"xt{t}")
                    for s in range(NT):
                        last = pe.transpose(bank[:, c(s)], x1[:, s, c(t)], ident[:])
                    last.then_inc(ring_a.fill(f"xt{t}"), 1)

            def qk(a, _):
                pe.wait_ge(x1t_hi_ready.sem, x1t_hi_ready.at(a, 2))
                pe.wait_ge(x1t_lo_ready.sem, x1t_lo_ready.at(a, 2))
                for name, hi, lo in (("q", wqt_hi, wqt_lo), ("k", wkt_hi, wkt_lo)):
                    for t in range(DT):
                        bank = take(ring_a, a, f"{name}{t}")
                        last = split_products(bank, [(hi[:, s, c(t)], lo[:, s, c(t)], x1t_hi[:, s, :], x1t_lo[:, s, :])
                                                     for s in range(DT)], C, C)
                        last.then_inc(ring_a.fill(f"{name}{t}"), 1)

            def make_values(a, _):
                for t in range(NT):
                    bank = take(ring_a, a, f"v{t}")
                    last = split_products(bank, [(x1t_hi[:, s, c(t)], x1t_lo[:, s, c(t)], wvt_hi[:, s, :], wvt_lo[:, s, :])
                                                 for s in range(DT)], D, D)
                    last.then_inc(ring_a.fill(f"v{t}"), 1)

            def attend(a, i):
                for kind, n in attention_parts(i, TILES):
                    name = f"{kind}{n}"
                    if kind == "s":
                        row, head = divmod(n, HEADS)
                        if n == 0:
                            pe.wait_ge(packed.sem, packed.at(a, packed.per))
                        bank = take(ring_a, a, name)
                        pe.matmul(bank[:], q_pack[:, head, c(row)], k_pack[:, head, :], start=True,
                                  stop=True).then_inc(ring_a.fill(name), 1)
                    elif kind == "t":
                        pe.wait_ge(probs_ready.sem, probs_ready.at(a, n + 1))
                        bank = take(ring_a, a, name)
                        for s in range(NT):
                            last = pe.transpose(bank[:, c(s)], probs[:, n % P_RING, c(s)], ident[:])
                        last.then_inc(ring_a.fill(name), 1)
                    elif kind == "c":
                        if n == 0:
                            pe.wait_ge(values_ready.sem, values_ready.at(a, 4))
                        both_pt_done(pe, a, GROUP * n + GROUP - 1)
                        pe.wait_ge(rrep_ready.sem, rrep_ready.at(a, n + 1))
                        bank = take(ring_a, a, name)
                        for s in range(NT):
                            for h in range(GROUP):
                                head = (n % 2) * GROUP + h
                                rows = slice(h * HEAD_DIM, (h + 1) * HEAD_DIM)
                                pe.matmul(bank[rows, 0:P], values[:, s, head * HEAD_DIM:(head + 1) * HEAD_DIM],
                                          probs_t[:, (GROUP * n + h) % PT_RING, s, :], start=s == 0, stop=s == NT - 1)
                        pe.transpose(bank[:, P:2 * P], recip_rep[:, n % 2, :], ident[:]).then_inc(ring_a.fill(name), 1)
                    else:
                        pe.wait_ge(cx_hi_ready.sem, cx_hi_ready.at(a, 2 * n + 2))
                        pe.wait_ge(cx_lo_ready.sem, cx_lo_ready.at(a, 2 * n + 2))
                        bank = take(ring_a, a, name)
                        last = split_products(bank, [(cx_hi[:, s, :], cx_lo[:, s, :], wot_hi[:, s, :], wot_lo[:, s, :])
                                                     for s in range(DT)], D, D)
                        last.then_inc(ring_a.fill(name), 1)

            def adj_t(b, t):
                bank = take(ring_b, b, f"at{t}")
                for s in range(NT):
                    last = pe.transpose(bank[:, c(s)], mask[:, s, c(t)], ident[:])
                last.then_inc(ring_b.fill(f"at{t}"), 1)

            def x2_t(b, _):
                pe.wait_ge(x2_ready.sem, x2_ready.at(b, 4))
                for t in range(DT):
                    bank = take(ring_b, b, f"xt{t}")
                    for s in range(NT):
                        last = pe.transpose(bank[:, c(s)], x2[:, s, c(t)], ident[:])
                    last.then_inc(ring_b.fill(f"xt{t}"), 1)

            def linear(b, t):
                if t == 0:
                    pe.wait_ge(xt_hi_ready.sem, xt_hi_ready.at(b, 2))
                    pe.wait_ge(xt_lo_ready.sem, xt_lo_ready.at(b, 2))
                bank = take(ring_b, b, f"l{t}")
                last = split_products(bank, [(xt_hi[:, s, c(t)], xt_lo[:, s, c(t)], l2t_hi[:, s, :], l2t_lo[:, s, :])
                                             for s in range(DT)], 2 * D, 2 * D)
                last.then_inc(ring_b.fill(f"l{t}"), 1)

            def spread(b, name, t, r_hi, r_lo, wide):
                bank = take(ring_b, b, f"{name}{t}")
                last = split_products(bank, [(adjt_hi[:, s, c(t)], adjt_lo[:, s, c(t)], r_hi[:, s, :], r_lo[:, s, :])
                                             for s in range(NT)], wide, D)
                last.then_inc(ring_b.fill(f"{name}{t}"), 1)

            def aggregate(b, t):
                if t == 0:
                    pe.wait_ge(adjt_hi_ready.sem, adjt_hi_ready.at(b, 4))
                    pe.wait_ge(adjt_lo_ready.sem, adjt_lo_ready.at(b, 4))
                    pe.wait_ge(y_hi_ready.sem, y_hi_ready.at(b, 4))
                    pe.wait_ge(y_lo_ready.sem, y_lo_ready.at(b, 4))
                spread(b, "n", t, y_hi, y_lo, D + 2)

            def x3_t(b, _):
                pe.wait_ge(x3_ready.sem, x3_ready.at(b, 4))
                for t in range(DT):
                    bank = take(ring_b, b, f"x3t{t}")
                    for s in range(NT):
                        last = pe.transpose(bank[:, c(s)], x3[:, s, c(t)], ident[:])
                    last.then_inc(ring_b.fill(f"x3t{t}"), 1)

            def mix(b, t):
                if t == 0:
                    pe.wait_ge(xt_hi_ready.sem, xt_hi_ready.at(b, 4))
                    pe.wait_ge(xt_lo_ready.sem, xt_lo_ready.at(b, 4))
                for name, lo_col, hi_col in ((f"ya{t}", 0, 2 * D), (f"yb{t}", 2 * D, MIX + 2)):
                    bank = take(ring_b, b, name)
                    w = hi_col - lo_col
                    last = split_products(bank, [(xt_hi[:, s, c(t)], xt_lo[:, s, c(t)], mix_hi[:, s, lo_col:hi_col],
                                                  mix_lo[:, s, lo_col:hi_col]) for s in range(DT)], w, w)
                    last.then_inc(ring_b.fill(name), 1)

            def source(b, _):
                bank = take(ring_b, b, "si")
                last = split_products(bank, [(urep_hi[:, s, :], urep_lo[:, s, :], xt_hi[:, s, :], xt_lo[:, s, :])
                                             for s in range(DT)], C, C)
                last.then_inc(ring_b.fill("si"), 1)

            def hop1(b, t):
                if t == 0:
                    pe.wait_ge(adjt_hi_ready.sem, adjt_hi_ready.at(b, 8))
                    pe.wait_ge(adjt_lo_ready.sem, adjt_lo_ready.at(b, 8))
                    pe.wait_ge(y_hi_ready.sem, y_hi_ready.at(b, 8))
                    pe.wait_ge(y_lo_ready.sem, y_lo_ready.at(b, 8))
                spread(b, "u", t, y_hi, y_lo, D + 2)

            def hop2(b, t):
                if t == 0:
                    pe.wait_ge(v_hi_ready.sem, v_hi_ready.at(b, 4))
                    pe.wait_ge(v_lo_ready.sem, v_lo_ready.at(b, 4))
                spread(b, "w", t, v_hi, v_lo, D)

            drive(pe, {("A", "incidence"): incidence, ("A", "to_edges"): to_edges, ("A", "degrees"): degrees,
                       ("A", "to_nodes"): to_nodes, ("A", "hidden"): hidden, ("A", "project"): project,
                       ("A", "to_edges2"): to_edges2, ("A", "to_nodes2"): to_nodes2, ("A", "x1_t"): x1_t,
                       ("A", "qk"): qk, ("A", "values"): make_values, ("A", "attend"): attend,
                       ("B", "adj_t"): adj_t, ("B", "x2_t"): x2_t, ("B", "linear"): linear,
                       ("B", "aggregate"): aggregate, ("B", "x3_t"): x3_t, ("B", "mix"): mix,
                       ("B", "source"): source, ("B", "hop1"): hop1, ("B", "hop2"): hop2})

        @block.scalar
        def _(act):
            copy = ACT.Copy

            def split_x(a, _):
                act.wait_ge(x_loaded.sem, x_loaded.at(a, 16))
                act_a.link(act, act.activation(x_hi[:, :, D:D + 2], ones[:, :].rearrange("p (a b) -> p a b", b=2), copy))
                act.activation(x_hi[:, :, 0:D], x_in[:], copy).then_inc(x_hi_ready.sem, 1)

            def scaled(a, name, t, n):
                act.wait_ge(ring_a.fill(name), ring_a.full(a, name))
                bank = ring_a.bank(name)
                act.wait_ge(be_ready.sem, be_ready.at(a, t + 1))
                act.activation(m_hi[:, t, :], bank[:, 0:D], copy, scale=be[:, t:t + 1]).then_inc(m_hi_ready.sem, 1)

            def to_edges(a, t):
                scaled(a, f"m{t}", t, t)

            def to_nodes(a, _):
                for t in range(DT):
                    act.wait_ge(g_ready.sem, g_ready.at(a, t + 1))
                    act.activation(g_hi[:, t, :], tmp_a[:, t, :], copy).then_inc(g_hi_ready.sem, 1)

            def hidden(a, t):
                act.wait_ge(ring_a.fill(f"h{t}"), ring_a.full(a, f"h{t}"))
                bank = ring_a.bank(f"h{t}")
                if t >= 2:
                    act.wait_ge(h_hi_ready.sem, h_hi_ready.at(a, t - 1))
                    act.wait_ge(h_lo_ready.sem, h_lo_ready.at(a, t - 1))
                else:
                    act.wait_ge(g_lo_ready.sem, g_lo_ready.at(a, 2))
                act.activation(tmp_a[:, t % 2, :], bank[:], ACT.Relu, bias=b1_col[:, t:t + 1]).then_inc(h_ready.sem, 1)
                act.wait_ge(h_ready.sem, h_ready.at(a, t + 1))
                act.activation(squares[:, t, :], tmp_a[:, t % 2, :], ACT.Square).then_inc(sq_ready.sem, 1)

            def project(a, _):
                for t in range(NT):
                    act.wait_ge(z_ready.sem, z_ready.at(a, t + 1))
                    act.activation(z_hi[:, t, :], tmp_a[:, t % 2, 0:D], copy).then_inc(z_hi_ready.sem, 1)

            def to_edges2(a, t):
                act.wait_ge(ring_a.fill(f"n{t}"), ring_a.full(a, f"n{t}"))
                bank = ring_a.bank(f"n{t}")
                act.activation(m_hi[:, t, :], bank[:, 0:D], copy, scale=be[:, t:t + 1]).then_inc(m_hi_ready.sem, 1)

            def x1_t(a, _):
                for t in range(DT):
                    act.wait_ge(ring_a.fill(f"xt{t}"), ring_a.full(a, f"xt{t}"))
                    bank = ring_a.bank(f"xt{t}")
                    act.activation(x1t_hi[:, t, :], bank[:], copy).then_inc(x1t_hi_ready.sem, 1)

            def qk(a, _):
                for name, dst, bias in (("q", q_hi, bq_col), ("k", k_hi, bk_col)):
                    for t in range(DT):
                        act.wait_ge(ring_a.fill(f"{name}{t}"), ring_a.full(a, f"{name}{t}"))
                        bank = ring_a.bank(f"{name}{t}")
                        act.activation(dst[:, t, :], bank[:], ACT.Identity, bias=bias[:, t:t + 1])\
                           .then_inc(qk_hi_ready.sem, 1)

            def attend(a, i):
                if 1 <= i <= TILES:
                    j = i - 1
                    act.wait_ge(top_ready.sem, top_ready.at(a, j + 1))
                    act.activation(probs[:, j % P_RING, :], probs[:, j % P_RING, :], ACT.Exp, bias=neg_top[:, j:j + 1],
                                   scale=SCALE2, accum_out=sums[:, j:j + 1]).then_inc(probs_ready.sem, 1)
                for kind, n in attention_parts(i, TILES):
                    if kind == "t" and n in on_scalar:
                        act.wait_ge(ring_a.fill(f"t{n}"), ring_a.full(a, f"t{n}"))
                        bank = ring_a.bank(f"t{n}")
                        act.activation(probs_t[:, n % PT_RING, :, :], bank[:].rearrange("p (s q) -> p s q", s=NT),
                                       copy).then_inc(pt_scalar.sem, 1)
                    if kind == "c":
                        act.wait_ge(ring_a.fill(f"c{n}"), ring_a.full(a, f"c{n}"))
                        bank = ring_a.bank(f"c{n}")
                        act.activation(recip_t[:, n % 2, :], bank[:, P:2 * P], copy).then_inc(rt_ready.sem, 1)
                        act.wait_ge(cx_ready.sem, cx_ready.at(a, n + 1))
                        act.activation(cx_hi[:, n % 2, :], tmp_a[:, n % 2, 0:P], copy).then_inc(cx_hi_ready.sem, 1)

            def adj_t(b, t):
                act.wait_ge(ring_b.fill(f"at{t}"), ring_b.full(b, f"at{t}"))
                bank = ring_b.bank(f"at{t}")
                act.activation(adjt_hi[:, t, :], bank[:], copy).then_inc(adjt_hi_ready.sem, 1)

            def turned(b, names, n):
                for t in range(DT):
                    act.wait_ge(ring_b.fill(f"{names}{t}"), ring_b.full(b, f"{names}{t}"))
                    bank = ring_b.bank(f"{names}{t}")
                    act.activation(xt_hi[:, t, :], bank[:], copy).then_inc(xt_hi_ready.sem, 1)

            def linear(b, t):
                act.wait_ge(ring_b.fill(f"l{t}"), ring_b.full(b, f"l{t}"))
                bank = ring_b.bank(f"l{t}")
                if t == 0:
                    act.wait_ge(stored.sem, stored.at(b, 16))
                act.activation(y_hi[:, t, 0:D], bank[:, D:2 * D], copy).then_inc(y_hi_ready.sem, 1)
                act.activation(y01[:, t, 0:D], bank[:, 0:D], copy).then_inc(y01_ready.sem, 1)

            def mix(b, t):
                act.wait_ge(ring_b.fill(f"ya{t}"), ring_b.full(b, f"ya{t}"))
                bank = ring_b.bank(f"ya{t}")
                act.activation(y01[:, t, D:2 * D], bank[:, D:2 * D], copy).then_inc(y01_ready.sem, 1)
                act.wait_ge(ring_b.fill(f"yb{t}"), ring_b.full(b, f"yb{t}"))
                bank = ring_b.bank(f"yb{t}")
                act.activation(y_hi[:, t, 0:D], bank[:, 0:D], copy).then_inc(y_hi_ready.sem, 1)

            def source(b, _):
                act.wait_ge(ring_b.fill("si"), ring_b.full(b, "si"))
                bank = ring_b.bank("si")
                act.activation(si_row[:], bank[:], copy).then_inc(si_ready.sem, 1)

            def alpha(b, t):
                act.wait_ge(lrelu_ready.sem, lrelu_ready.at(b, t + 1))
                act.activation(e_tmp[:], e_tmp[:], ACT.Exp).then_inc(exp_ready.sem, 1)
                act.wait_ge(alpha_ready.sem, alpha_ready.at(b, t + 1))
                act.activation(adjt_hi[:, t, :], al_tmp[:], copy).then_inc(adjt_hi_ready.sem, 1)

            def hop1(b, t):
                act.wait_ge(v_ready.sem, v_ready.at(b, t + 1))
                act.activation(v_hi[:, t, :], v_tmp[:], copy).then_inc(v_hi_ready.sem, 1)

            drive(act, {("A", "split_x"): split_x, ("A", "to_edges"): to_edges, ("A", "to_nodes"): to_nodes,
                        ("A", "hidden"): hidden, ("A", "project"): project, ("A", "to_edges2"): to_edges2,
                        ("A", "x1_t"): x1_t, ("A", "qk"): qk, ("A", "attend"): attend,
                        ("B", "adj_t"): adj_t, ("B", "x2_t"): lambda b, n: turned(b, "xt", 0),
                        ("B", "linear"): linear, ("B", "x3_t"): lambda b, n: turned(b, "x3t", 2),
                        ("B", "mix"): mix, ("B", "source"): source, ("B", "alpha"): alpha, ("B", "hop1"): hop1},
                  chains["act"])

        @block.gpsimd
        def _(pool):
            def minus(dst, src, hi):
                return pool.tensor_tensor(dst, src, plain(hi), ALU.subtract)

            def split_x(a, _):
                pool.wait_ge(x_hi_ready.sem, x_hi_ready.at(a, 1))
                minus(x_lo[:], x_in[:], x_hi[:, :, 0:D]).then_inc(x_lo_ready.sem, 1)
                pool.wait_ge(x_lo_ready.sem, x_lo_ready.at(a, 1))
                pool_a.link(pool, pool.tensor_tensor(x_in[:], x_in[:], x_in[:], ALU.add))
                for t in range(NT):
                    last = pool.tensor_tensor(x_in[:, t, :], x_in[:, t, :], b2_row[:], ALU.add)
                last.then_inc(x2b_ready.sem, 1)

            def to_nodes(a, _):
                for t in range(DT):
                    pool.wait_ge(g_hi_ready.sem, g_hi_ready.at(a, t + 1))
                    minus(g_lo[:, t, :], tmp_a[:, t, :], g_hi[:, t, :]).then_inc(g_lo_ready.sem, 1)

            def hidden(a, t):
                pool.wait_ge(h_hi_ready.sem, h_hi_ready.at(a, t + 1))
                minus(h_lo[:, t, :], tmp_a[:, t % 2, :], h_hi[:, t, :]).then_inc(h_lo_ready.sem, 1)

            def inverse_root(dst, src, n):
                return pool.tensor_tensor(dst, src, half_neg[:, 0:n], ALU.pow)

            def project(a, _):
                pool.wait_ge(var_ready.sem, var_ready.at(a, 1))
                settle(pool, "pool")
                inverse_root(stat[:, 4, :], stat[:, 3, :], NT).then_inc(rstd_ready.sem, 1)
                for t in range(NT):
                    pool.wait_ge(z_hi_ready.sem, z_hi_ready.at(a, t + 1))
                    settle(pool, "pool")
                    minus(z_lo[:, t, :], tmp_a[:, t % 2, 0:D], z_hi[:, t, :]).then_inc(z_lo_ready.sem, 1)

            def to_nodes2(a, _):
                pool.wait_ge(var_ready.sem, var_ready.at(a, 2))
                inverse_root(rs_a[:], ve_a[:], NT).then_inc(rstd_ready.sem, 1)

            def make_values(a, _):
                pool.wait_ge(x1t_lo_ready.sem, x1t_lo_ready.at(a, 2))
                for t in range(NT):
                    last = pool.tensor_tensor(x1[:, t, :], x1[:, t, :], bo_row[:], ALU.add)
                last.then_inc(x1b_ready.sem, 1)

            def attend(a, i):
                for kind, n in attention_parts(i, TILES):
                    if kind == "c":
                        pool.wait_ge(cx_hi_ready.sem, cx_hi_ready.at(a, n + 1))
                        minus(cx_lo[:, n % 2, :], tmp_a[:, n % 2, 0:P], cx_hi[:, n % 2, :]).then_inc(cx_lo_ready.sem, 1)
                    if kind == "o":
                        pool.wait_ge(var_ready.sem, var_ready.at(a, 3 + n))
                        inverse_root(rs_a[:, n:n + 1], ve_a[:, n:n + 1], 1).then_inc(rstd_ready.sem, 1)

            def norm2(b, _):
                pool.wait_ge(var_b.sem, var_b.at(b, 1))
                inverse_root(rs_b[:], ve_b[:], NT).then_inc(rstd_b.sem, 1)

            def alpha(b, t):
                if t > 0:
                    pool.wait_ge(adjt_lo_ready.sem, adjt_lo_ready.at(b, 4 + t))
                    pool.wait_ge(adjt_hi_ready.sem, adjt_hi_ready.at(b, 4 + t))
                pool.wait_ge(y_hi_ready.sem, y_hi_ready.at(b, 8))
                pool.wait_ge(adjt_hi_ready.sem, adjt_hi_ready.at(b, 4 + t))
                pool_b.link(pool, pool.tensor_tensor(al_tmp[:], plain(adjt_hi[:, t, :]), plain(adjt_lo[:, t, :]), ALU.add))
                pool.wait_ge(exp_ready.sem, exp_ready.at(b, t + 1))
                pool.tensor_tensor(al_tmp[:], al_tmp[:], e_tmp[:], ALU.mult).then_inc(alpha_ready.sem, 1)
                pool.wait_ge(adjt_hi_ready.sem, adjt_hi_ready.at(b, 5 + t))
                minus(adjt_lo[:, t, :], al_tmp[:], adjt_hi[:, t, :]).then_inc(adjt_lo_ready.sem, 1)

            def hop1(b, t):
                pool.wait_ge(v_hi_ready.sem, v_hi_ready.at(b, t + 1))
                minus(v_lo[:, t, :], v_tmp[:], v_hi[:, t, :]).then_inc(v_lo_ready.sem, 1)

            def norm3(b, _):
                pool.wait_ge(var_b.sem, var_b.at(b, 2))
                inverse_root(rs_b[:], ve_b[:], NT).then_inc(rstd_b.sem, 1)

            drive(pool, {("A", "split_x"): split_x, ("A", "to_nodes"): to_nodes, ("A", "hidden"): hidden,
                         ("A", "project"): project, ("A", "to_nodes2"): to_nodes2, ("A", "values"): make_values,
                         ("A", "attend"): attend, ("B", "norm2"): norm2, ("B", "alpha"): alpha,
                         ("B", "hop1"): hop1, ("B", "norm3"): norm3}, chains["pool"])

        @block.vector
        def _(dve):
            dve.sem_inc(stored.sem, 16)

            def link_a(ins):
                chain_a.link(dve, ins)

            def link_b(ins):
                chain_b.link(dve, ins)

            def low(dst, src, hi):
                return dve.tensor_tensor(dst, src, plain(hi), ALU.subtract)

            def stats(link, bn, mv, ve, t, src):
                link(dve.bn_stats(bn[:, t, :], src))
                settle(dve, "vector")
                link(dve.bn_aggr(mv[:, t, :], bn[:, t, :]))
                return dve.tensor_scalar(ve[:, t:t + 1], mv[:, t, 1:2], LN_EPS, None, ALU.add)

            def normal(dst, src, mv, rs, t):
                return dve.tensor_scalar(dst, src, mv[:, t, 0:1], rs[:, t:t + 1], ALU.subtract, ALU.mult)

            def incidence(a, _):
                dve.wait_ge(adj_in.sem, adj_in.at(a, 16))
                for t in range(NT):
                    dve.tensor_scalar(inc[:, t, :], mask[:, t, :], 0.0, None, ALU.not_equal).then_inc(inc_ready.sem, 1)
                for t in range(NT):
                    dve.wait_ge(ring_a.fill(f"ht{t}"), ring_a.full(a, f"ht{t}"))
                    bank = ring_a.bank(f"ht{t}")
                    dve.tensor_copy(w_col[:, t:t + 1], bank[:, 0:1])
                    dve.tensor_scalar(inc_t[:, t, :], bank[:], 0.0, None, ALU.not_equal).then_inc(inc_t_ready.sem, 1)
                dve.wait_ge(inc_t_ready.sem, inc_t_ready.at(a, NT))
                link_a(dve.tensor_copy(w_hl[:, :, 0], w_col[:]))
                link_a(low(w_hl[:, :, 1], w_col[:], w_hl[:, :, 0]))
                dve.tensor_copy(w_rep_hi[:], plain(w_hl[:, :, 0:1]).to_broadcast([P, NT, P]))
                dve.tensor_copy(w_rep_lo[:], plain(w_hl[:, :, 1:2]).to_broadcast([P, NT, P])).then_inc(w_ready.sem, 1)

            def to_edges(a, t):
                dve.wait_ge(ring_a.fill(f"m{t}"), ring_a.full(a, f"m{t}"))
                bank = ring_a.bank(f"m{t}")
                link_a(dve.tensor_scalar(be_t[:, t:t + 1], bank[:, D:D + 1], 0.5, None, ALU.max))
                dve.reciprocal(be[:, t:t + 1], be_t[:, t:t + 1]).then_inc(be_ready.sem, 1)
                dve.wait_ge(m_hi_ready.sem, m_hi_ready.at(a, t + 1))
                dve.scalar_tensor_tensor(out=m_lo[:, t, :], in0=bank[:, 0:D], scalar=be[:, t:t + 1],
                                         in1=plain(m_hi[:, t, :]), op0=ALU.mult, op1=ALU.subtract)\
                   .then_inc(m_lo_ready.sem, 1)

            def degrees(a, _):
                dve.wait_ge(ring_a.fill("dcol"), ring_a.full(a, "dcol"))
                bank = ring_a.bank("dcol")
                pair = bank[:, 0:2 * NT].rearrange("p (t k) -> p t k", k=2)
                link_a(dve.tensor_copy(dn_t[:, 0, :], pair[:, :, 0]))
                dve.tensor_tensor(dn_t[:, 0, :], pair[:, :, 1], dn_t[:, 0, :], ALU.add).then_inc(dcol_read.sem, 1)
                dve.wait_ge(dcol_read.sem, dcol_read.at(a, 1))
                link_a(dve.tensor_scalar(dn_t[:, 1, :], dn_t[:, 0, :], TINY, None, ALU.max))
                link_a(dve.reciprocal(dn_t[:, 1, :], dn_t[:, 1, :]))
                link_a(dve.scalar_tensor_tensor(out=dn[:], in0=dn_t[:, 0, :], scalar=0.0, in1=dn_t[:, 1, :],
                                                op0=ALU.is_gt, op1=ALU.mult))
                dve.wait_ge(ring_a.fill("drow"), ring_a.full(a, "drow"))
                bank = ring_a.bank("drow")
                link_a(dve.tensor_scalar(dn_row[:], bank[:], TINY, None, ALU.max))
                link_a(dve.reciprocal(dn_row[:], dn_row[:]))
                dve.scalar_tensor_tensor(out=dn_row[:], in0=bank[:], scalar=0.0, in1=dn_row[:],
                                         op0=ALU.is_gt, op1=ALU.mult).then_inc(drow_ready.sem, 1)

            def to_nodes(a, _):
                dve.wait_ge(drow_ready.sem, drow_ready.at(a, 1))
                for t in range(DT):
                    dve.wait_ge(ring_a.fill(f"g{t}"), ring_a.full(a, f"g{t}"))
                    bank = ring_a.bank(f"g{t}")
                    dve.tensor_tensor(tmp_a[:, t, :], bank[:], dn_row[:], ALU.mult).then_inc(g_ready.sem, 1)

            def hidden(a, t):
                dve.wait_ge(h_ready.sem, h_ready.at(a, t + 1))
                dve.tensor_copy(h_hi[:, t, :], tmp_a[:, t % 2, :]).then_inc(h_hi_ready.sem, 1)

            def project(a, _):
                for t in range(NT):
                    dve.wait_ge(ring_a.fill(f"z{t}"), ring_a.full(a, f"z{t}"))
                    bank = ring_a.bank(f"z{t}")
                    link_a(dve.tensor_scalar(stat[:, 0, t:t + 1], bank[:, D:D + 1], 1.0 / DH, None, ALU.mult))
                    link_a(dve.tensor_scalar(stat[:, 1, t:t + 1], bank[:, D + 4:D + 5], 1.0 / DH, None, ALU.mult))
                link_a(dve.tensor_tensor(stat[:, 2, :], stat[:, 0, :], stat[:, 0, :], ALU.mult))
                link_a(dve.tensor_tensor(stat[:, 3, :], stat[:, 1, :], stat[:, 2, :], ALU.subtract))
                dve.tensor_scalar(stat[:, 3, :], stat[:, 3, :], 0.0, LN_EPS, ALU.max, ALU.add).then_inc(var_ready.sem, 1)
                dve.wait_ge(rstd_ready.sem, rstd_ready.at(a, 1))
                for t in range(NT):
                    bank = ring_a.bank(f"z{t}")
                    if t >= 2:
                        dve.wait_ge(z_lo_ready.sem, z_lo_ready.at(a, t - 1))
                    dve.scalar_tensor_tensor(out=tmp_a[:, t % 2, 0:D], in0=bank[:, 0:D], scalar=stat[:, 4, t:t + 1],
                                             in1=betaw2_row[:], op0=ALU.mult, op1=ALU.add).then_inc(z_ready.sem, 1)

            def to_edges2(a, t):
                dve.wait_ge(ring_a.fill(f"n{t}"), ring_a.full(a, f"n{t}"))
                bank = ring_a.bank(f"n{t}")
                dve.wait_ge(m_hi_ready.sem, m_hi_ready.at(a, NT + t + 1))
                dve.scalar_tensor_tensor(out=m_lo[:, t, :], in0=bank[:, 0:D], scalar=be[:, t:t + 1],
                                         in1=plain(m_hi[:, t, :]), op0=ALU.mult, op1=ALU.subtract)\
                   .then_inc(m_lo_ready.sem, 1)

            def to_nodes2(a, _):
                dve.wait_ge(x2b_ready.sem, x2b_ready.at(a, 1))
                for t in range(NT):
                    dve.wait_ge(ring_a.fill(f"y{t}"), ring_a.full(a, f"y{t}"))
                    bank = ring_a.bank(f"y{t}")
                    dve.scalar_tensor_tensor(out=x1[:, t, :], in0=bank[:, 0:D], scalar=dn[:, t:t + 1],
                                             in1=x_in[:, t, :], op0=ALU.mult, op1=ALU.add).then_inc(y_read.sem, 1)
                    dve.wait_ge(y_read.sem, y_read.at(a, t + 1))
                    last = stats(link_a, bn_a, mv_a, ve_a, t, x1[:, t, :])
                last.then_inc(var_ready.sem, 1)
                dve.wait_ge(rstd_ready.sem, rstd_ready.at(a, 2))
                for t in range(NT):
                    normal(x1[:, t, :], x1[:, t, :], mv_a, rs_a, t).then_inc(x1_ready.sem, 1)

            def x1_t(a, _):
                for t in range(DT):
                    bank = ring_a.bank(f"xt{t}")
                    dve.wait_ge(x1t_hi_ready.sem, x1t_hi_ready.at(a, t + 1))
                    low(x1t_lo[:, t, :], bank[:], x1t_hi[:, t, :]).then_inc(x1t_lo_ready.sem, 1)

            def qk(a, _):
                for n, (name, hi, lo, bias) in enumerate((("q", q_hi, q_lo, bq_col), ("k", k_hi, k_lo, bk_col))):
                    for t in range(DT):
                        bank = ring_a.bank(f"{name}{t}")
                        dve.wait_ge(qk_hi_ready.sem, qk_hi_ready.at(a, 2 * n + t + 1))
                        dve.scalar_tensor_tensor(out=lo[:, t, :], in0=bank[:], scalar=bias[:, t:t + 1],
                                                 in1=plain(hi[:, t, :]), op0=ALU.add, op1=ALU.subtract)\
                           .then_inc(qk_lo_ready.sem, 1)

            def make_values(a, _):
                for t in range(NT):
                    dve.wait_ge(ring_a.fill(f"v{t}"), ring_a.full(a, f"v{t}"))
                    bank = ring_a.bank(f"v{t}")
                    dve.tensor_tensor(values[:, t, :], bank[:, 0:D], bv_row[:], ALU.add).then_inc(values_ready.sem, 1)

            def attend(a, i):
                if i < TILES:
                    dve.wait_ge(ring_a.fill(f"s{i}"), ring_a.full(a, f"s{i}"))
                    bank = ring_a.bank(f"s{i}")
                    settle(dve, "vector")
                    dve.tensor_tensor_reduce(probs[:, i % P_RING, :], bank[:], mask[:, i // HEADS, :], 1.0, -3.4e38,
                                             ALU.mult, ALU.max, top[:, i:i + 1]).then_inc(masked.sem, 1)
                if 1 <= i <= TILES:
                    dve.wait_ge(masked.sem, masked.at(a, i))
                    dve.tensor_scalar(neg_top[:, i - 1:i], top[:, i - 1:i], -SCALE2, None, ALU.mult)\
                       .then_inc(top_ready.sem, 1)
                for kind, n in attention_parts(i, TILES):
                    if kind == "t" and n in on_vector:
                        dve.wait_ge(ring_a.fill(f"t{n}"), ring_a.full(a, f"t{n}"))
                        bank = ring_a.bank(f"t{n}")
                        dve.tensor_copy(probs_t[:, n % PT_RING, :, :], bank[:].rearrange("p (s q) -> p s q", s=NT))\
                           .then_inc(pt_vector.sem, 1)
                    if kind == "c":
                        dve.wait_ge(rt_ready.sem, rt_ready.at(a, n + 1))
                        dve.tensor_tensor(tmp_a[:, n % 2, 0:P], ring_a.bank(f"c{n}")[:, 0:P], recip_t[:, n % 2, :],
                                          ALU.mult).then_inc(cx_ready.sem, 1)
                    if kind == "o":
                        if n == 0:
                            dve.wait_ge(x1b_ready.sem, x1b_ready.at(a, 1))
                        dve.wait_ge(ring_a.fill(f"o{n}"), ring_a.full(a, f"o{n}"))
                        bank = ring_a.bank(f"o{n}")
                        dve.tensor_tensor(x2[:, n, :], bank[:, 0:D], x1[:, n, :], ALU.add).then_inc(o_read.sem, 1)
                        dve.wait_ge(o_read.sem, o_read.at(a, n + 1))
                        stats(link_a, bn_a, mv_a, ve_a, n, x2[:, n, :]).then_inc(var_ready.sem, 1)
                        dve.wait_ge(rstd_ready.sem, rstd_ready.at(a, 3 + n))
                        normal(x2[:, n, :], x2[:, n, :], mv_a, rs_a, n).then_inc(x2_ready.sem, 1)
                if i >= 6 and (i - 6) % GROUP == 0 and (i - 6) // GROUP < TILES // GROUP:
                    n = (i - 6) // GROUP
                    dve.wait_ge(probs_ready.sem, probs_ready.at(a, GROUP * n + GROUP))
                    four = slice(GROUP * n, GROUP * n + GROUP)
                    link_a(dve.reciprocal(rsum[:, four], sums[:, four]))
                    dve.tensor_copy(recip_rep[:, n % 2, :].rearrange("p (h d) -> p h d", h=GROUP),
                                    rsum[:, four].rearrange("p (h o) -> p h o", o=1).to_broadcast([P, GROUP, HEAD_DIM]))\
                       .then_inc(rrep_ready.sem, 1)

            def adj_t(b, t):
                dve.wait_ge(adjt_hi_ready.sem, adjt_hi_ready.at(b, t + 1))
                low(adjt_lo[:, t, :], ring_b.bank(f"at{t}")[:], adjt_hi[:, t, :]).then_inc(adjt_lo_ready.sem, 1)

            def turned(b, names, n):
                for t in range(DT):
                    dve.wait_ge(xt_hi_ready.sem, xt_hi_ready.at(b, n + t + 1))
                    low(xt_lo[:, t, :], ring_b.bank(f"{names}{t}")[:], xt_hi[:, t, :]).then_inc(xt_lo_ready.sem, 1)

            def linear(b, t):
                dve.wait_ge(y_hi_ready.sem, y_hi_ready.at(b, t + 1))
                dve.wait_ge(y01_ready.sem, y01_ready.at(b, t + 1))
                low(y_lo[:, t, :], ring_b.bank(f"l{t}")[:, D:2 * D], y_hi[:, t, 0:D]).then_inc(y_lo_ready.sem, 1)

            def aggregate(b, t):
                dve.wait_ge(ring_b.fill(f"n{t}"), ring_b.full(b, f"n{t}"))
                bank = ring_b.bank(f"n{t}")
                link_b(dve.tensor_scalar(bdeg[:, 0, t:t + 1], bank[:, D:D + 1], DEG_EPS, None, ALU.max))
                link_b(dve.reciprocal(bdeg[:, 1, t:t + 1], bdeg[:, 0, t:t + 1]))
                dve.scalar_tensor_tensor(out=x3[:, t, :], in0=bank[:, 0:D], scalar=bdeg[:, 1, t:t + 1],
                                         in1=y01[:, t, 0:D], op0=ALU.mult, op1=ALU.add).then_inc(n_read.sem, 1)
                dve.wait_ge(n_read.sem, n_read.at(b, t + 1))
                link_b(dve.scalar_tensor_tensor(out=x3[:, t, :], in0=x3[:, t, :], scalar=0.0, in1=x2[:, t, :],
                                                op0=ALU.max, op1=ALU.add))
                last = stats(link_b, bn_b, mv_b, ve_b, t, x3[:, t, :])
                if t == NT - 1:
                    last.then_inc(var_b.sem, 1)

            def norm2(b, _):
                dve.wait_ge(rstd_b.sem, rstd_b.at(b, 1))
                for t in range(NT):
                    normal(x3[:, t, :], x3[:, t, :], mv_b, rs_b, t).then_inc(x3_ready.sem, 1)

            def mix(b, t):
                dve.wait_ge(y01_ready.sem, y01_ready.at(b, NT + t + 1))
                dve.tensor_tensor(y01[:, t, 0:D], ring_b.bank(f"ya{t}")[:, 0:D], bm_row[:], ALU.add)\
                   .then_inc(y0_ready.sem, 1)
                dve.wait_ge(y_hi_ready.sem, y_hi_ready.at(b, NT + t + 1))
                bank = ring_b.bank(f"yb{t}")
                dve.tensor_tensor(sj_col[:, t:t + 1], bank[:, D:D + 1], shift_col, ALU.add).then_inc(sj_ready.sem, 1)
                low(y_lo[:, t, :], bank[:, 0:D], y_hi[:, t, 0:D]).then_inc(y_lo_ready.sem, 1)

            def alpha(b, t):
                if t == 0:
                    dve.wait_ge(si_ready.sem, si_ready.at(b, 1))
                    dve.wait_ge(sj_ready.sem, sj_ready.at(b, 4))
                else:
                    dve.wait_ge(alpha_ready.sem, alpha_ready.at(b, t))
                link_b(dve.tensor_scalar(e_tmp[:], si_row[:], sj_col[:, t:t + 1], None, ALU.add))
                dve.scalar_tensor_tensor(out=e_tmp[:], in0=e_tmp[:], scalar=0.2, in1=e_tmp[:], op0=ALU.mult,
                                         op1=ALU.max).then_inc(lrelu_ready.sem, 1)

            def hop1(b, t):
                dve.wait_ge(ring_b.fill(f"u{t}"), ring_b.full(b, f"u{t}"))
                bank = ring_b.bank(f"u{t}")
                link_b(dve.tensor_scalar(bdeg[:, 0, t:t + 1], bank[:, D:D + 1], SUM_EPS, None, ALU.add))
                link_b(dve.reciprocal(bdeg[:, 1, t:t + 1], bdeg[:, 0, t:t + 1]))
                if t >= 1:
                    dve.wait_ge(v_lo_ready.sem, v_lo_ready.at(b, t))
                dve.scalar_tensor_tensor(out=v_tmp[:], in0=bank[:, 0:D], scalar=bdeg[:, 1, t:t + 1],
                                         in1=y01[:, t, D:2 * D], op0=ALU.mult, op1=ALU.add).then_inc(v_ready.sem, 1)

            def hop2(b, t):
                dve.wait_ge(ring_b.fill(f"w{t}"), ring_b.full(b, f"w{t}"))
                bank = ring_b.bank(f"w{t}")
                dve.wait_ge(y0_ready.sem, y0_ready.at(b, t + 1))
                dve.scalar_tensor_tensor(out=y01[:, t, 0:D], in0=bank[:, 0:D], scalar=bdeg[:, 1, t:t + 1],
                                         in1=y01[:, t, 0:D], op0=ALU.mult, op1=ALU.add).then_inc(w_read.sem, 1)
                dve.wait_ge(w_read.sem, w_read.at(b, t + 1))
                link_b(dve.scalar_tensor_tensor(out=y01[:, t, 0:D], in0=y01[:, t, 0:D], scalar=0.0, in1=x3[:, t, :],
                                                op0=ALU.max, op1=ALU.add))
                last = stats(link_b, bn_b, mv_b, ve_b, t, y01[:, t, 0:D])
                if t == NT - 1:
                    last.then_inc(var_b.sem, 1)

            def norm3(b, _):
                dve.wait_ge(rstd_b.sem, rstd_b.at(b, 2))
                for t in range(NT):
                    last = normal(y01[:, t, 0:D], y01[:, t, 0:D], mv_b, rs_b, t)
                last.then_inc(out_ready.sem, 1)

            drive(dve, {("A", "incidence"): incidence, ("A", "to_edges"): to_edges, ("A", "degrees"): degrees,
                        ("A", "to_nodes"): to_nodes, ("A", "hidden"): hidden, ("A", "project"): project,
                        ("A", "to_edges2"): to_edges2, ("A", "to_nodes2"): to_nodes2, ("A", "x1_t"): x1_t,
                        ("A", "qk"): qk, ("A", "values"): make_values, ("A", "attend"): attend,
                        ("B", "adj_t"): adj_t, ("B", "x2_t"): lambda b, n: turned(b, "xt", 0),
                        ("B", "linear"): linear, ("B", "aggregate"): aggregate, ("B", "norm2"): norm2,
                        ("B", "x3_t"): lambda b, n: turned(b, "x3t", 2), ("B", "mix"): mix, ("B", "alpha"): alpha,
                        ("B", "hop1"): hop1, ("B", "hop2"): hop2, ("B", "norm3"): norm3}, chains["dve"])


_INS = ["x", "adj", "L0_gnn_W1", "L0_gnn_b1", "L0_gnn_gamma", "L0_gnn_beta", "L0_gnn_W2", "L0_gnn_b2", "L1_gnn_Wq",
        "L1_gnn_bq", "L1_gnn_Wk", "L1_gnn_bk", "L1_gnn_Wv", "L1_gnn_bv", "L1_gnn_Wo", "L1_gnn_bo", "L2_gnn_W",
        "L3_gnn_Wv", "L3_gnn_bv", "L3_gnn_aw", "L3_gnn_ab", "L3_gnn_Wk", "L3_gnn_bk"]


def kernel(**inputs):
    import numpy as _np
    import concourse.bacc as _bacc
    from concourse import mybir as _mybir
    from concourse.bass_utils import run_bass_kernel_spmd as _run

    nc = _bacc.Bacc("TRN2", target_bir_lowering=False, num_devices=1)
    arrays, args = {}, []
    for name in _INS:
        a = _np.ascontiguousarray(inputs[name])
        arrays[f"in_{name}_dram"] = a
        args.append(nc.dram_tensor(f"in_{name}_dram", a.shape, _mybir.dt.from_np(a.dtype), kind="ExternalInput").ap())
    shape = tuple(inputs["x"].shape)
    args.append(nc.dram_tensor("out_0_dram", shape, _mybir.dt.from_np(_np.dtype("float32")), kind="ExternalOutput").ap())
    build(nc, *args)
    r = _run(nc, [arrays], core_ids=[0])
    return r.results[0]["out_0_dram"]
```

```python
from contextlib import ExitStack

import concourse.bass as bass
from concourse import mybir

F32 = mybir.dt.float32
F32R = mybir.dt.float32r
ACT = mybir.ActivationFunctionType
ALU = mybir.AluOpType

P = 128
HEADS = 8
HEAD_DIM = 32
GROUP = P // HEAD_DIM
PACKED = 3 * HEAD_DIM
TINY = 1.1754944e-38
LN_EPS = 1e-5
DEG_EPS = 1e-6
SUM_EPS = 1e-12
LEAK = 0.2
A_BANKS, B_BANKS = 6, 2
EARLY = 12
SCORE_BANKS = 2
P_RING = 4
PT_RING = 8
EVAC_ON_VECTOR = (2, 6)
AT_STEPS = (19, 21, 23, 25)
TAIL = 33
STEPS = 48


class Batch:

    def __init__(self, reg, offset):
        self.reg, self.offset = reg, offset

    def at(self, per, n):
        if self.reg is None:
            return self.offset * per + n
        return self.reg * per + (self.offset * per + n)

    def index(self):
        return self.offset if self.reg is None else (self.reg if not self.offset else self.reg + self.offset)

    def first(self):
        return self.reg is None and self.offset == 0

    def before(self):
        return Batch(self.reg, self.offset - 1)


class Signal:

    def __init__(self, sem, per):
        self.sem, self.per = sem, per

    def at(self, batch, n):
        return batch.at(self.per, n)


class Chain:

    def __init__(self, sem, per):
        self.sem, self.per, self.n, self.batch = sem, per, 0, None

    def begin(self, batch):
        assert self.n in (0, self.per), (self.n, self.per)
        self.batch, self.n = batch, 0

    def link(self, eng, ins):
        self.n += 1
        ins.then_inc(self.sem, 1)
        eng.wait_ge(self.sem, self.batch.at(self.per, self.n))


class Ring:

    def __init__(self, banks, results, filled):
        self.banks, self.filled, self.read = banks, filled, {}
        self.held = [[name for name, k in results if k == bank] for bank in range(len(banks))]
        self.place = {name: (k, self.held[k].index(name)) for name, k in results}

    def bank(self, name):
        return self.banks[self.place[name][0]]

    def fill(self, name):
        return self.filled[self.place[name][0]]

    def full(self, batch, name):
        k, use = self.place[name]
        return batch.at(len(self.held[k]), use + 1)

    def occupant(self, batch, name):
        k, use = self.place[name]
        if use > 0:
            return self.held[k][use - 1], batch
        return (None, None) if batch.first() else (self.held[k][-1], batch.before())


def attention_parts(i, tiles):
    parts = []
    if i < tiles:
        parts.append(("s", i))
    if i >= 9 and (i - 8) % 4 and (i - 8) // 4 < tiles // 4:
        parts.append((f"c{(i - 8) % 4}", (i - 8) // 4))
    if 3 <= i < tiles + 3:
        parts.append(("t", i - 3))
    if i >= 8 and (i - 8) % 4 == 0 and (i - 8) // 4 < tiles // 4:
        parts += [("r", (i - 8) // 4), ("c0", (i - 8) // 4)]
    if i >= 18 and (i - 18) % 8 == 0 and (i - 18) // 8 < tiles // 8:
        parts.append(("o", (i - 18) // 8))
    if i in AT_STEPS:
        parts.append(("at", AT_STEPS.index(i)))
    return parts


def every(i, first, step, count):
    n, off = divmod(i - first, step)
    return n if not off and 0 <= n < count else None


def in_turn(names, banks):
    return [(name, banks[i % len(banks)]) for i, name in enumerate(names)]


def a_results(tiles):
    names = [f"ht{t}" for t in range(4)] + [f"m{t}" for t in range(4)] + ["dcol", "g0", "drow", "g1"]
    names += [f"h{t}" for t in range(4)] + [f"z{t}" for t in range(4)]
    names += [f"n{t}" for t in range(4)] + [f"y{t}" for t in range(4)] + ["xt0", "xt1"]
    names += ["q0", "q1", "k0", "k1"] + [f"v{t}" for t in range(4)]
    results = in_turn(names[:EARLY], range(SCORE_BANKS)) + in_turn(names[EARLY:], range(A_BANKS))
    parts = [part for i in range(STEPS) for part in attention_parts(i, tiles)]
    results += in_turn([f"s{n}" for kind, n in parts if kind == "s"], range(SCORE_BANKS))
    results += in_turn([f"{kind}{n}" for kind, n in parts if kind in ("t", "r", "o", "at")],
                       range(SCORE_BANKS, A_BANKS - 1))
    return results + in_turn([f"c{n}" for kind, n in parts if kind == "c0"], [A_BANKS - 1])


def b_results():
    names = ["xt0", "xt1"] + [f"l{t}" for t in range(4)]
    names += [f"n{t}" for t in range(4)] + ["x3t0", "x3t1"]
    for t in range(4):
        names += [f"ya{t}", f"yb{t}"]
    return in_turn(names + ["si"] + [f"u{t}" for t in range(4)] + [f"w{t}" for t in range(4)], range(B_BANKS))


def round_schedule():
    def a(name, *ns):
        order.extend(("A", name, n) for n in ns)

    def b(name, *ns):
        order.extend(("B", name, n) for n in ns)

    order = []
    a("load", 0), a("inc_rows", 0), b("attend", 33, 34), a("split_x", 0), a("inc_rows", 1, 2), b("attend", 35, 36)
    a("inc_rows", 3), a("incidence", 0), a("residual0", 0), a("to_edges", 0), b("attend", 37, 38), a("to_edges", 1)
    b("attend", 39, 40, 41), a("to_edges", 2, 3), b("attend", 42), a("degrees", 0), b("attend", *range(43, 48))
    a("to_nodes", 0), b("x2_t", 0), b("x2_split", 0), b("linear", 0), b("linear_out", 0), b("linear", 1, 2)
    b("linear_out", 1), b("linear", 3), a("hidden", 0), b("linear_out", 2, 3), a("hidden", 1, 2, 3)
    b("aggregate", 0, 1), b("agg_sum", 0, 1), b("agg_stats", 0), a("project", 0), b("agg_stats", 1)
    b("aggregate", 2), b("agg_sum", 2), a("rescale", 0), b("aggregate", 3), b("agg_sum", 3), b("agg_stats", 2, 3)
    b("norm2", 0), b("merge", 0), a("to_edges2", 0, 1, 2), b("merge", 1), a("to_edges2", 3), b("merge", 2, 3)
    b("x3_t", 0), b("x3_split", 0), a("to_nodes2", 0), b("mix", 0), b("mix_out", 0), b("mix", 1), a("normal1", 0)
    b("mix_out", 1), b("mix", 2), b("mix_out", 2), a("x1_t", 0), b("mix", 3), b("mix_out", 3), b("source", 0)
    b("source_out", 0), a("qk", 0), b("alpha_exp", 0, 1), b("alpha_split", 0, 1), b("alpha_exp", 2, 3)
    b("alpha_split", 2, 3), a("values", 0), b("hop1", 0), b("hop1_out", 0), b("hop1", 1), b("hop1_out", 1)
    b("hop1", 2), b("hop1_out", 2), b("hop1", 3), b("hop1_out", 3), a("attend", 0, 1, 2), b("hop2", 0)
    a("attend", 3, 4), b("hop2", 1), b("hop2_sum", 0), a("attend", 5, 6), b("hop2", 2), b("hop2_stats", 0)
    a("attend", 7), b("hop2_sum", 1), a("attend", 8, 9, 10), b("hop2_sum", 2), a("attend", 11), b("hop2_stats", 1)
    b("hop2", 3), a("attend", 12), b("hop2_sum", 3), a("attend", 13, 14), b("hop2_stats", 2, 3), a("attend", 15, 16)
    b("norm3", 0), a("attend", *range(17, 33))
    return order


def build(nc, x, adj, W1, b1, gamma, beta, W2, b2, Wq, bq, Wk, bk, Wv, bv, Wo, bo, L2W,
          Pv, pbv, aw, ab, Wm, bm, out):
    BATCH, C, D = x.shape
    DH = W1.shape[0]
    K3 = Wm.shape[0]
    NT, DT, HT_ = C // P, D // P, DH // P
    TILES = NT * HEADS
    SCALE2 = 2.0 * HEAD_DIM ** -0.5
    MIX = K3 * D
    assert (C, D, DH, K3, HEADS * HEAD_DIM) == (512, 256, 512, 3, D)

    ctx = ExitStack()
    with ctx:
        cursor = [(nc.sbuf_base + 31) // 32 * 32]

        def place(name, shape, dt, at=None):
            size = 4
            for s in shape[1:]:
                size *= s
            size = (size + 31) // 32 * 32
            if at is None:
                at = cursor[0]
                cursor[0] += size
            assert at + size <= nc.sbuf_usable_end, (name, at + size)
            return nc.alloc_sbuf_tensor_at(name, shape, dt, offset=at)

        def sem(name):
            return ctx.enter_context(nc.semaphore(name))

        def signal(name, per):
            return Signal(sem(name), per)

        w1t_hi, w1t_lo = (place(f"w1t_{s}", [P, DT, DH], F32R) for s in ("hi", "lo"))
        w2c_hi = place("w2c_hi", [P, HT_, D + 2], F32R)
        w2c_lo = place("w2c_lo", [P, HT_, D], F32R)
        wqt_hi, wqt_lo = (place(f"wqt_{s}", [P, DT, D], F32R) for s in ("hi", "lo"))
        wkt_hi, wkt_lo = (place(f"wkt_{s}", [P, DT, D], F32R) for s in ("hi", "lo"))
        wvt_hi, wvt_lo = (place(f"wvt_{s}", [P, DT, D], F32R) for s in ("hi", "lo"))
        wot_hi, wot_lo = (place(f"wot_{s}", [P, DT, D], F32R) for s in ("hi", "lo"))
        l2t_hi, l2t_lo = (place(f"l2t_{s}", [P, DT, 2 * D], F32R) for s in ("hi", "lo"))
        mix_hi, mix_lo = (place(f"mix_{s}", [P, DT, MIX + 2], F32R) for s in ("hi", "lo"))
        urep_hi, urep_lo = (place(f"urep_{s}", [P, DT, P], F32R) for s in ("hi", "lo"))
        b2_row = place("b2_row", [P, D], F32)
        betaw2_row = place("betaw2_row", [P, D], F32)
        bv_row = place("bv_row", [P, D], F32)
        bo_row = place("bo_row", [P, D], F32)
        bm_row = place("bm_row", [P, D], F32)
        ident = place("ident", [P, P], F32)
        ones = place("ones", [P, 8], F32)
        half_neg = place("half_neg", [P, 4], F32)
        cols = place("cols", [P, 24], F32)
        b1_col, gamma_col, beta_col = cols[:, 0:4], cols[:, 4:8], cols[:, 8:12]
        bq_col, bk_col, shift_col = cols[:, 12:14], cols[:, 14:16], cols[:, 16:17]

        weights_end = cursor[0]

        at = cursor[0]
        cursor[0] += 16384
        inc = place("inc", [P, NT, C], F32R, at)
        inc_t = place("inc_t", [P, NT, C], F32R, at + 8192)
        q_pack = place("q_pack", [P, HEADS, C], F32R, at)
        at = cursor[0]
        cursor[0] += 16384
        h_hi = place("h_hi", [P, HT_, C], F32R, at)
        h_lo = place("h_lo", [P, HT_, C], F32R, at + 8192)
        k_pack = place("k_pack", [P, HEADS, C], F32R, at)
        at = cursor[0]
        cursor[0] += 16384
        m_hi = place("m_hi", [P, NT, D], F32R, at)
        m_lo = place("m_lo", [P, NT, D], F32R, at + 4096)
        g_hi = place("g_hi", [P, DT, C], F32R, at + 8192)
        g_lo = place("g_lo", [P, DT, C], F32R, at + 12288)
        q_hi = place("q_hi", [P, DT, C], F32R, at)
        q_lo = place("q_lo", [P, DT, C], F32R, at + 4096)
        k_hi = place("k_hi", [P, DT, C], F32R, at + 8192)
        k_lo = place("k_lo", [P, DT, C], F32R, at + 12288)
        probs_t = place("probs_t", [P, PT_RING, NT, P], F32, at)
        at = cursor[0]
        cursor[0] += 8224
        x_hi = place("x_hi", [P, NT, D + 2], F32R, at)
        x_lo = place("x_lo", [P, NT, D], F32R, at + 4128)
        z_hi = place("z_hi", [P, NT, D], F32R, at)
        z_lo = place("z_lo", [P, NT, D], F32R, at + 4128)
        x1t_hi = place("x1t_hi", [P, DT, C], F32R, at)
        x1t_lo = place("x1t_lo", [P, DT, C], F32R, at + 4128)
        mask_at = cursor[0]
        mask = place("mask", [P, NT, C], F32)
        x_in = place("x_in", [P, NT, D], F32)
        x1 = place("x1", [P, NT, D], F32)
        values = place("values", [P, NT, D], F32)
        at = probs_at = cursor[0]
        cursor[0] += 8192
        probs = place("probs", [P, P_RING, C], F32, at)
        squares = place("squares", [P, HT_, C], F32, at)
        e_small = place("e_small", [P, 2, C], F32, at)
        dn_rep = place("dn_rep", [P, NT, P], F32, at)
        dn_row = place("dn_row", [P, C], F32, at + 4096)
        tmp_a = place("tmp_a", [P, 2, C], F32)
        recip_rep = place("recip_rep", [P, 2, P], F32)

        recip_t = place("recip_t", [P, 2, P], F32)
        cx_hi = place("cx_hi", [P, DT, P], F32R)
        cx_lo = place("cx_lo", [P, DT, P], F32R)
        w_col = place("w_col", [P, NT], F32)
        w_hl = place("w_hl", [P, NT, 2], F32R)
        be = place("be", [P, NT], F32)
        be_t = place("be_t", [P, NT], F32)
        dn = place("dn", [P, NT], F32)
        dn_t = place("dn_t", [P, 2, NT], F32)
        stat = place("stat", [P, 5, NT], F32)
        bn_a = place("bn_a", [P, NT, 6], F32)
        mv_a = place("mv_a", [P, NT, 2], F32)
        ve_a = place("ve_a", [P, NT], F32)
        rs_a = place("rs_a", [P, NT], F32)
        top = place("top", [P, TILES], F32)
        neg_top = place("neg_top", [P, TILES], F32)
        sums = place("sums", [P, TILES], F32)
        rsum = place("rsum", [P, TILES], F32)

        at = cursor[0]
        cursor[0] += 16384
        adjt_hi = place("adjt_hi", [P, NT, C], F32R, at)
        adjt_lo = place("adjt_lo", [P, NT, C], F32R, at + 8192)
        adj_whole = place("adj_whole", [P, NT, C], F32, at)
        alpha_whole = place("alpha_whole", [P, NT, C], F32, at + 8192)
        x2 = place("x2", [P, NT, D], F32)
        x3 = place("x3", [P, NT, D], F32)
        at = cursor[0]
        cursor[0] += 8192
        xt_hi = place("xt_hi", [P, DT, C], F32R, at)
        xt_lo = place("xt_lo", [P, DT, C], F32R, at + 4096)
        v_hi = place("v_hi", [P, NT, D], F32R, at)
        v_lo = place("v_lo", [P, NT, D], F32R, at + 4096)
        y01 = place("y01", [P, NT, 2 * D], F32)
        y_hi = place("y_hi", [P, NT, D + 2], F32R)
        y_lo = place("y_lo", [P, NT, D], F32R)
        at = cursor[0]
        si_row = place("si_row", [P, C], F32)
        cx_tmp = place("cx_tmp", [P, 2, P], F32, at)
        at = cursor[0]
        e_tmp = place("e_tmp", [P, 2, C], F32)
        v_tmp = place("v_tmp", [P, 2, D], F32, at)
        sj_col = place("sj_col", [P, NT], F32)
        sj_small = place("sj_small", [P, NT], F32)
        bdeg = place("bdeg", [P, 2, NT], F32)
        bn_b = place("bn_b", [P, NT, 6], F32)
        mv_b = place("mv_b", [P, NT, 2], F32)
        ve_b = place("ve_b", [P, NT], F32)
        rs_b = place("rs_b", [P, NT], F32)

        banks = [ctx.enter_context(nc.psum_tensor(f"bank{k}", [P, 512], F32)) for k in range(8)]

        ring_a = Ring(banks[:A_BANKS], a_results(TILES), [sem(f"a_filled{k}") for k in range(A_BANKS)])
        ring_b = Ring(banks[A_BANKS:A_BANKS + B_BANKS], b_results(), [sem(f"b_filled{k}") for k in range(B_BANKS)])

        def plain(ap):
            return ap.bitcast(F32)

        adj_in, x_loaded = [signal(f"adj_in{t}", 16) for t in range(NT)], signal("x_loaded", 16)
        prepare(nc, ctx, locals())
        rounds(nc, ctx, locals())


def prepare(nc, ctx, v):
    g = dict(v)
    (place, sem, banks, ident, ones, cols, plain) = (g[k] for k in ("place", "sem", "banks", "ident", "ones", "cols", "plain"))
    DT, HT_, D, DH, MIX, K3, C = (g[k] for k in ("DT", "HT_", "D", "DH", "MIX", "K3", "C"))
    spot = [g["weights_end"]]

    def staged(name, shape, dt=F32):
        size = 4
        for s in shape[1:]:
            size *= s
        at = spot[0]
        spot[0] += (size + 31) // 32 * 32
        return nc.alloc_sbuf_tensor_at(name, shape, dt, offset=at)

    w1n = staged("w1n", [P, HT_, D])
    w2n = staged("w2n", [P, DT, DH])
    wn = {n: staged(f"{n}_n", [P, DT, D]) for n in ("q", "k", "v", "o")}
    l2n = staged("l2n", [P, DT, 2 * D])
    w2t = staged("w2t", [P, HT_, D])
    mixn = staged("mixn", [P, DT, MIX + 2])
    pvn = staged("pvn", [P, DT, D])
    aw_row = staged("aw_row", [P, 2 * D])
    pbv_row = staged("pbv_row", [P, D])
    bm_rows = staged("bm_rows", [P, K3 * D])
    gamma_rep = staged("gamma_rep", [P, HT_, P])
    beta_rep = staged("beta_rep", [P, HT_, P])
    u_rep = staged("u_rep", [P, DT, P])
    dots = staged("dots", [P, 8])
    assert spot[0] <= g["mask_at"]
    spot[0] = g["probs_at"]
    w2s = staged("w2s", [P, HT_, D])
    junk = staged("junk", [P, 6, D])
    loaded = sem("weights_loaded")
    const = sem("constants_ready")
    turned = sem("weights_turned")
    high = sem("weights_high")
    low = sem("weights_low")
    reps = sem("weights_rep")
    chain = sem("weights_chain")
    rows = sem("weights_rows")

    items = []
    for t in range(DT):
        items.append(([w1n[:, s, t * P:(t + 1) * P] for s in range(HT_)], g["w1t_hi"][:, t, :], g["w1t_lo"][:, t, :]))
    for n in ("q", "k", "v", "o"):
        for t in range(DT):
            items.append(([wn[n][:, s, t * P:(t + 1) * P] for s in range(DT)],
                          g[f"w{n}t_hi"][:, t, :], g[f"w{n}t_lo"][:, t, :]))
    for t in range(DT):
        items.append(([l2n[:, s, half * D + t * P:half * D + (t + 1) * P] for half in range(2) for s in range(DT)],
                      g["l2t_hi"][:, t, :], g["l2t_lo"][:, t, :]))
    n_split = len(items)
    for t in range(HT_):
        items.append(([w2n[:, s, t * P:(t + 1) * P] for s in range(DT)], w2t[:, t, :], None))

    def col(vec, n):
        return vec.rearrange("(t p) -> p t", p=P)

    loads = [
        (w1n[:], g["W1"].rearrange("(t p) d -> p t d", p=P)),
        (wn["q"][:], g["Wq"].rearrange("(t p) d -> p t d", p=P)),
        (wn["k"][:], g["Wk"].rearrange("(t p) d -> p t d", p=P)),
        (wn["v"][:], g["Wv"].rearrange("(t p) d -> p t d", p=P)),
        (wn["o"][:], g["Wo"].rearrange("(t p) d -> p t d", p=P)),
        (l2n[:], g["L2W"].rearrange("(t p) d -> p t d", p=P)),
        (w2n[:], g["W2"].rearrange("(t p) d -> p t d", p=P)),
        (pvn[:], g["Pv"].rearrange("(t p) d -> p t d", p=P)),
        (aw_row[:], g["aw"].rearrange("a b -> (a b)").partition_broadcast(P)),
        (pbv_row[:], g["pbv"].partition_broadcast(P)),
        (bm_rows[:], g["bm"].rearrange("k d -> (k d)").partition_broadcast(P)),
        (g["b2_row"][:], g["b2"].partition_broadcast(P)),
        (g["bv_row"][:], g["bv"].partition_broadcast(P)),
        (g["bo_row"][:], g["bo"].partition_broadcast(P)),
        (cols[:, 17:18], g["ab"].partition_broadcast(P)),
    ] + [(mixn[:, :, k * D:(k + 1) * D], g["Wm"][k].rearrange("(t p) d -> p t d", p=P)) for k in range(K3)]
    small = [(g["b1_col"], g["b1"]), (g["gamma_col"], g["gamma"]), (g["beta_col"], g["beta"]),
             (g["bq_col"], g["bq"]), (g["bk_col"], g["bk"])]

    with nc.Block() as block:
        @block.sync
        def _(sp):
            for dst, src in loads:
                sp.dma_start(dst, src).then_inc(loaded, 16)
            with nc.allow_non_contiguous_dma(reason="bias vectors, once"):
                for dst, src in small:
                    sp.dma_start(dst, col(src, 0)).then_inc(loaded, 16)
            sp.dma_start(g["x_in"][:], g["x"][0].rearrange("(t p) d -> p t d", p=P)).then_inc(g["x_loaded"].sem, 16)
            for t in range(C // P):
                sp.dma_start(g["mask"][:, t, :], g["adj"][0, t * P:(t + 1) * P, :]).then_inc(g["adj_in"][t].sem, 16)
            sp.wait_ge(loaded, 16 * (len(loads) + len(small)))

        @block.gpsimd
        def _(pool):
            pool.memset(ident[:], 0.0).then_inc(const, 1)
            pool.memset(ones[:], 1.0).then_inc(const, 1)
            pool.memset(g["half_neg"][:], -0.5).then_inc(const, 1)
            pool.wait_ge(const, 3)
            pool.affine_select(out=ident[:], in_=ident[:], compare_op=ALU.not_equal, fill=1.0, base=0,
                               pattern=[[-1, P]], channel_multiplier=1).then_inc(const, 1)

        @block.tensor
        def _(pe):
            pe.wait_ge(const, 4)
            pe.wait_ge(loaded, 16 * (len(loads) + len(small)))
            for n, (srcs, hi, lo) in enumerate(items):
                if n >= 8:
                    pe.wait_ge(low, n - 7)
                for s, src in enumerate(srcs):
                    last = pe.transpose(banks[n % 8][:, s * P:(s + 1) * P], src, ident[:])
                last.then_inc(turned, 1)
            pe.wait_ge(low, len(items))
            pe.wait_ge(reps, 1)
            for n, rep in enumerate((gamma_rep, beta_rep)):
                for t in range(HT_):
                    last = pe.matmul(banks[n][:, 0:D], rep[:, t, :], w2t[:, t, :], start=t == 0, stop=t == HT_ - 1)
                last.then_inc(turned, 1)

        @block.scalar
        def _(act):
            for n, (srcs, hi, lo) in enumerate(items):
                act.wait_ge(turned, n + 1)
                act.activation(hi, banks[n % 8][:, 0:len(srcs) * P], ACT.Copy).then_inc(high, 1)
            act.wait_ge(turned, len(items) + 2)
            act.activation(g["betaw2_row"][:], banks[1][:, 0:D], ACT.Copy).then_inc(rows, 1)
            act.wait_ge(const, 4)
            for t in range(HT_):
                act.activation(g["w2c_hi"][:, t, D:D + 2], ones[:, 0:2], ACT.Copy).then_inc(rows, 1)
                act.activation(g["y_hi"][:, t, D:D + 2], ones[:, 0:2], ACT.Copy).then_inc(rows, 1)

        @block.vector
        def _(dve):
            count = [0]

            def link(ins):
                count[0] += 1
                ins.then_inc(chain, 1)
                dve.wait_ge(chain, count[0])

            dve.wait_ge(loaded, 16 * (len(loads) + len(small)))
            dve.wait_ge(const, 4)
            for t in range(HT_):
                dve.tensor_scalar(gamma_rep[:, t, :], ones[:, 0:1].to_broadcast([P, P]), g["gamma_col"][:, t:t + 1],
                                  1.0 / DH, ALU.mult, ALU.mult)
                last = dve.tensor_scalar(beta_rep[:, t, :], ones[:, 0:1].to_broadcast([P, P]),
                                         g["beta_col"][:, t:t + 1], None, ALU.mult)
            last.then_inc(reps, 1)
            for n, (srcs, hi, lo) in enumerate(items):
                dve.wait_ge(high, n + 1)
                if lo is None:
                    dve.tensor_copy(dots[:, 4:5], ones[:, 0:1]).then_inc(low, 1)
                    dve.wait_ge(low, n + 1)
                else:
                    dve.tensor_tensor(lo, banks[n % 8][:, 0:len(srcs) * P], plain(hi), ALU.subtract).then_inc(low, 1)
            dve.wait_ge(turned, len(items) + 1)
            for t in range(HT_):
                link(dve.scalar_tensor_tensor(out=w2s[:, t, :], in0=w2t[:, t, :], scalar=g["gamma_col"][:, t:t + 1],
                                              in1=banks[0][:, 0:D], op0=ALU.mult, op1=ALU.subtract))
                link(dve.tensor_copy(g["w2c_hi"][:, t, 0:D], w2s[:, t, :]))
                link(dve.tensor_tensor(g["w2c_lo"][:, t, :], w2s[:, t, :], plain(g["w2c_hi"][:, t, 0:D]), ALU.subtract))
            for t in range(DT):
                for s in range(2):
                    link(dve.tensor_tensor_reduce(junk[:, 2 * t + s, :], pvn[:, t, :], aw_row[:, s * D:(s + 1) * D], 1.0, 0.0,
                                                  ALU.mult, ALU.add, dots[:, 2 * t + s:2 * t + s + 1]))
                link(dve.tensor_copy(mixn[:, t, MIX:MIX + 2], dots[:, 2 * t:2 * t + 1].to_broadcast([P, 2])))
                link(dve.tensor_scalar(u_rep[:, t, :], ones[:, 0:1].to_broadcast([P, P]),
                                       dots[:, 2 * t + 1:2 * t + 2], None, ALU.mult))
            for s in range(2):
                link(dve.tensor_tensor_reduce(junk[:, 4 + s, :], pbv_row[:], aw_row[:, s * D:(s + 1) * D], 1.0, 0.0,
                                              ALU.mult, ALU.add, dots[:, 6 + s:7 + s]))
            link(dve.tensor_tensor(dots[:, 5:6], dots[:, 6:7], dots[:, 7:8], ALU.add))
            link(dve.tensor_tensor(g["shift_col"], dots[:, 5:6], cols[:, 17:18], ALU.add))
            link(dve.tensor_copy(g["mix_hi"][:], mixn[:]))
            link(dve.tensor_tensor(g["mix_lo"][:], mixn[:], plain(g["mix_hi"][:]), ALU.subtract))
            link(dve.tensor_copy(g["urep_hi"][:], u_rep[:]))
            link(dve.tensor_tensor(g["urep_lo"][:], u_rep[:], plain(g["urep_hi"][:]), ALU.subtract))
            link(dve.tensor_tensor(g["bm_row"][:], bm_rows[:, 0:D], bm_rows[:, D:2 * D], ALU.add))
            link(dve.tensor_tensor(g["bm_row"][:], g["bm_row"][:], bm_rows[:, 2 * D:3 * D], ALU.add))


def rounds(nc, ctx, v):
    names = ("adj_in x_loaded signal sem ring_a ring_b plain ident ones half_neg b1_col bq_col bk_col shift_col b2_row betaw2_row "
             "bv_row bo_row bm_row w1t_hi w1t_lo w2c_hi w2c_lo wqt_hi wqt_lo wkt_hi wkt_lo wvt_hi wvt_lo wot_hi "
             "wot_lo l2t_hi l2t_lo mix_hi mix_lo urep_hi urep_lo inc inc_t q_pack k_pack h_hi h_lo m_hi m_lo g_hi "
             "g_lo q_hi q_lo k_hi k_lo probs_t x_hi x_lo z_hi z_lo x1t_hi x1t_lo mask x_in x1 values probs squares "
             "cx_tmp adj_whole alpha_whole e_small sj_small dn_rep dn_row tmp_a recip_rep recip_t cx_hi cx_lo w_col w_hl be be_t dn dn_t stat bn_a "
             "mv_a ve_a rs_a top neg_top sums rsum adjt_hi adjt_lo x2 x3 xt_hi xt_lo v_hi v_lo y01 y_hi y_lo "
             "si_row e_tmp v_tmp sj_col bdeg bn_b mv_b ve_b rs_b x adj out BATCH C D DH NT DT HT_ TILES "
             "SCALE2 MIX")
    (adj_in, x_loaded, signal, sem, ring_a, ring_b, plain, ident, ones, half_neg, b1_col, bq_col, bk_col, shift_col, b2_row, betaw2_row,
     bv_row, bo_row, bm_row, w1t_hi, w1t_lo, w2c_hi, w2c_lo, wqt_hi, wqt_lo, wkt_hi, wkt_lo, wvt_hi, wvt_lo, wot_hi,
     wot_lo, l2t_hi, l2t_lo, mix_hi, mix_lo, urep_hi, urep_lo, inc, inc_t, q_pack, k_pack, h_hi, h_lo, m_hi, m_lo,
     g_hi, g_lo, q_hi, q_lo, k_hi, k_lo, probs_t, x_hi, x_lo, z_hi, z_lo, x1t_hi, x1t_lo, mask, x_in, x1, values,
     probs, squares, cx_tmp, adj_whole, alpha_whole, e_small, sj_small, dn_rep, dn_row, tmp_a, recip_rep, recip_t, cx_hi, cx_lo, w_col, w_hl, be, be_t, dn,
     dn_t, stat, bn_a, mv_a, ve_a, rs_a, top, neg_top, sums, rsum, adjt_hi, adjt_lo, x2, x3, xt_hi, xt_lo, v_hi,
     v_lo, y01, y_hi, y_lo, si_row, e_tmp, v_tmp, sj_col, bdeg, bn_b, mv_b, ve_b, rs_b, x, adj, out, BATCH,
     C, D, DH, NT, DT, HT_, TILES, SCALE2, MIX) = (v[k] for k in names.split())

    settled = {e: sem(f"settled_{e}") for e in ("sp", "pool", "vector", "tensor")}

    inc_ready, inc_t_ready = signal("inc_ready", 4), signal("inc_t_ready", 4)
    w_ready = signal("w_ready", 1)
    x_hi_ready, x_lo_ready, x2b_ready = signal("x_hi_ready", 1), signal("x_lo_ready", 1), signal("x2b_ready", 1)
    be_ready = signal("be_ready", 4)
    m_hi_ready, m_lo_ready = signal("m_hi_ready", 8), signal("m_lo_ready", 8)
    g_ready, g_hi_ready, g_lo_ready = signal("g_ready", 2), signal("g_hi_ready", 2), signal("g_lo_ready", 2)
    h_ready, h_hi_ready, h_lo_ready = signal("h_ready", 4), signal("h_hi_ready", 4), signal("h_lo_ready", 4)
    sq_ready, sq_summed = signal("sq_ready", 4), signal("sq_summed", 3)
    var_ready, rstd_ready = signal("var_ready", 6), signal("rstd_ready", 6)
    z_ready, z_hi_ready, z_lo_ready = signal("z_ready", 4), signal("z_hi_ready", 4), signal("z_lo_ready", 4)
    x1_ready, x1b_ready = signal("x1_ready", 4), signal("x1b_ready", 1)
    x1t_hi_ready, x1t_lo_ready = signal("x1t_hi_ready", 2), signal("x1t_lo_ready", 2)
    qk_hi_ready, qk_lo_ready = signal("qk_hi_ready", 4), signal("qk_lo_ready", 4)
    values_ready = signal("values_ready", 4)
    packed = [signal(f"packed{h}", 16 * 2 * 3) for h in range(GROUP)]
    masked, top_ready = signal("masked", TILES), signal("top_ready", TILES)
    probs_ready = signal("probs_ready", TILES)
    on_vector = [i for i in range(TILES) if i % HEADS in EVAC_ON_VECTOR]
    on_scalar = [i for i in range(TILES) if i % HEADS not in EVAC_ON_VECTOR]
    pt_vector, pt_scalar = signal("pt_vector", len(on_vector)), signal("pt_scalar", len(on_scalar))
    rrep_ready, rt_ready = signal("rrep_ready", 8), signal("rt_ready", 8)
    cx_ready, cx_hi_ready, cx_lo_ready = signal("cx_ready", 8), signal("cx_hi_ready", 8), signal("cx_lo_ready", 8)
    x2_ready = signal("x2_ready", 4)
    adjt_hi_ready, adjt_lo_ready = signal("adjt_hi_ready", 8), signal("adjt_lo_ready", 8)
    xt_hi_ready, xt_lo_ready = signal("xt_hi_ready", 4), signal("xt_lo_ready", 4)
    y_hi_ready, y_lo_ready, y01_ready = signal("y_hi_ready", 8), signal("y_lo_ready", 8), signal("y01_ready", 8)
    var_b, rstd_b = signal("var_b", 2), signal("rstd_b", 2)
    x3_ready = signal("x3_ready", 4)
    sj_sum = signal("sj_sum", 4)
    sj_ready, si_ready, lrelu_ready, exp_ready = (signal("sj_ready", 4), signal("si_ready", 1),
                                                  signal("lrelu_ready", 4), signal("exp_ready", 4))
    merged, alpha_ready = signal("merged", 4), signal("alpha_ready", 4)
    rsum_ready, o_stats, o_moments = signal("rsum_ready", 8), signal("o_stats", 4), signal("o_moments", 4)
    dn_rep_ready = signal("dn_rep_ready", 1)
    dcol_read, drow_ready = signal("dcol_read", 1), signal("drow_ready", 1)
    y_read, o_read, n_read, w_read = (signal(f"{k}_read", 4) for k in "yonw")
    y_stats, y_moments = signal("y_stats", 4), signal("y_moments", 4)
    x3_sum, b_stats, b_moments = signal("x3_sum", 4), signal("b_stats", 8), signal("b_moments", 8)
    y0_ready, hop2_done = signal("y0_ready", 4), signal("hop2_done", 4)
    v_ready, v_hi_ready, v_lo_ready = signal("v_ready", 4), signal("v_hi_ready", 4), signal("v_lo_ready", 4)
    out_ready, stored = signal("out_ready", 1), signal("stored", 16)
    chain_a, chain_b = Chain(sem("vector_chain_a"), 19), Chain(sem("vector_chain_b"), 16)
    pool_a, act_a = Chain(sem("pool_chain_a"), 1), Chain(sem("scalar_chain_a"), 1)
    chains = {"dve": (chain_a, chain_b), "pool": (pool_a, None), "act": (act_a, None)}

    def settle(eng, who):
        eng.sem_inc(settled[who], 1)

    def pt_done(eng, a, i):
        if i in on_vector:
            eng.wait_ge(pt_vector.sem, pt_vector.at(a, on_vector.index(i) + 1))
        else:
            eng.wait_ge(pt_scalar.sem, pt_scalar.at(a, on_scalar.index(i) + 1))

    def both_pt_done(eng, a, i):
        nv, ns = sum(j <= i for j in on_vector), sum(j <= i for j in on_scalar)
        if nv:
            eng.wait_ge(pt_vector.sem, pt_vector.at(a, nv))
        if ns:
            eng.wait_ge(pt_scalar.sem, pt_scalar.at(a, ns))

    for t in range(4):
        ring_a.read.update({f"ht{t}": (inc_t_ready, t + 1), f"m{t}": (m_lo_ready, t + 1), f"h{t}": (h_ready, t + 1),
                            f"z{t}": (z_ready, t + 1), f"n{t}": (m_lo_ready, NT + t + 1), f"y{t}": (y_read, t + 1),
                            f"v{t}": (values_ready, t + 1), f"o{t}": (o_read, t + 1),
                            f"at{t}": (adjt_lo_ready, t + 1)})
        ring_b.read.update({f"l{t}": (y_lo_ready, t + 1), f"n{t}": (n_read, t + 1),
                            f"ya{t}": (y0_ready, t + 1), f"yb{t}": (y_lo_ready, NT + t + 1),
                            f"u{t}": (v_ready, t + 1), f"w{t}": (w_read, t + 1)})
    for t in range(2):
        ring_a.read.update({f"g{t}": (g_ready, t + 1), f"xt{t}": (x1t_lo_ready, t + 1), f"q{t}": (qk_lo_ready, t + 1),
                            f"k{t}": (qk_lo_ready, DT + t + 1)})
        ring_b.read.update({f"xt{t}": (xt_lo_ready, t + 1), f"x3t{t}": (xt_lo_ready, DT + t + 1)})
    ring_a.read.update(dcol=(dcol_read, 1), drow=(drow_ready, 1))
    ring_b.read.update(si=(si_ready, 1))
    for i in range(TILES):
        ring_a.read[f"s{i}"] = (masked, i + 1)
        ring_a.read[f"t{i}"] = (pt_vector, on_vector.index(i) + 1) if i in on_vector else \
                               (pt_scalar, on_scalar.index(i) + 1)
    for n in range(TILES // GROUP):
        ring_a.read[f"r{n}"] = (rt_ready, n + 1)
        ring_a.read[f"c{n}"] = (cx_ready, n + 1)


    order = round_schedule()

    def drive(eng, stages, links=(None, None)):
        def one(a, b):
            for c, batch in zip(links, (a, b)):
                if c is not None and batch is not None:
                    c.begin(batch)
            for thread, name, n in order:
                batch = a if thread == "A" else b
                if batch is not None and (thread, name) in stages:
                    stages[thread, name](batch, n)

        one(Batch(None, 0), None)
        one(Batch(None, 1), Batch(None, 0))
        with eng.Fori(2, BATCH) as r:
            one(Batch(r, 0), Batch(r, -1))
        one(None, Batch(None, BATCH - 1))

    with nc.Block() as block:
        @block.sync
        def _(sp):
            def load(a, _):
                if a.first():
                    return
                sp.wait_ge(x1_ready.sem, x1_ready.at(a.before(), 4))
                settle(sp, "sp")
                sp.dma_start(x_in[:], x[a.index()].rearrange("(t p) d -> p t d", p=P)).then_inc(x_loaded.sem, 16)
                rows = adj[a.index()].rearrange("(t p) c -> p t c", p=P)
                sp.wait_ge(adjt_hi_ready.sem, adjt_hi_ready.at(a.before(), 4))
                settle(sp, "sp")
                for t in range(NT):
                    sp.wait_ge(masked.sem, masked.at(a.before(), (t + 1) * HEADS))
                    settle(sp, "sp")
                    sp.dma_start(mask[:, t, :], rows[:, t, :]).then_inc(adj_in[t].sem, 16)

            def qk(a, _):
                def move(hi, lo, pack, blocks, h):
                    rows = slice(h * HEAD_DIM, (h + 1) * HEAD_DIM)
                    for block_row, part in enumerate(blocks):
                        to = slice(block_row * HEAD_DIM, (block_row + 1) * HEAD_DIM)
                        sp.dma_start(plain(pack[to, h:HEADS:GROUP, :]), plain((hi, lo)[part][rows, :, :]))\
                          .then_inc(packed[h].sem, 16)

                sp.wait_ge(qk_hi_ready.sem, qk_hi_ready.at(a, 2))
                sp.wait_ge(qk_lo_ready.sem, qk_lo_ready.at(a, 2))
                settle(sp, "sp")
                for h in range(2):
                    move(q_hi, q_lo, q_pack, (0, 1, 0), h)
                sp.wait_ge(qk_hi_ready.sem, qk_hi_ready.at(a, 4))
                sp.wait_ge(qk_lo_ready.sem, qk_lo_ready.at(a, 4))
                settle(sp, "sp")
                for h in range(GROUP):
                    if h >= 2:
                        move(q_hi, q_lo, q_pack, (0, 1, 0), h)
                    move(k_hi, k_lo, k_pack, (0, 0, 1), h)

            def norm3(b, _):
                sp.wait_ge(out_ready.sem, out_ready.at(b, 1))
                settle(sp, "sp")
                sp.dma_start(out[b.index()].rearrange("(t p) d -> p t d", p=P), y01[:, :, 0:D]).then_inc(stored.sem, 16)

            drive(sp, {("A", "load"): load, ("A", "qk"): qk, ("B", "norm3"): norm3})
            sp.wait_ge(stored.sem, 16 * BATCH + 16)

        @block.tensor
        def _(pe):
            def take(ring, batch, name):
                before, its_batch = ring.occupant(batch, name)
                if before is not None:
                    signal_of, n = ring.read[before]
                    pe.wait_ge(signal_of.sem, signal_of.at(its_batch, n))
                return ring.bank(name)

            def add_products(bank, l_hi, l_lo, r_hi, r_lo, wide, width, first, final):
                pe.matmul(bank[:, 0:wide], l_hi, r_hi, start=first, stop=False)
                pe.matmul(bank[:, 0:wide], l_lo, r_hi, start=False, stop=False)
                return pe.matmul(bank[:, 0:width], l_hi, r_lo, start=False, stop=final)

            def split_products(bank, parts, wide, width):
                for n, part in enumerate(parts):
                    last = add_products(bank, *part, wide, width, n == 0, n == len(parts) - 1)
                return last

            def c(t):
                return slice(t * P, (t + 1) * P)

            def incidence(a, _):
                for t in range(NT):
                    bank = take(ring_a, a, f"ht{t}")
                    for s in range(NT):
                        if t == 0:
                            pe.wait_ge(adj_in[s].sem, adj_in[s].at(a, 16))
                        last = pe.transpose(bank[:, c(s)], mask[:, s, c(t)], ident[:])
                    last.then_inc(ring_a.fill(f"ht{t}"), 1)

            def to_edges(a, t):
                if t == 0:
                    pe.wait_ge(inc_ready.sem, inc_ready.at(a, NT))
                    pe.wait_ge(x_hi_ready.sem, x_hi_ready.at(a, 1))
                    pe.wait_ge(x_lo_ready.sem, x_lo_ready.at(a, 1))
                bank = take(ring_a, a, f"m{t}")
                for s in range(NT):
                    pe.matmul(bank[:, 0:D + 2], inc[:, s, c(t)], x_hi[:, s, :], start=s == 0, stop=False)
                    last = pe.matmul(bank[:, 0:D], inc[:, s, c(t)], x_lo[:, s, :], start=False, stop=s == NT - 1)
                last.then_inc(ring_a.fill(f"m{t}"), 1)

            def degrees(a, _):
                pe.wait_ge(w_ready.sem, w_ready.at(a, 1))
                bank = take(ring_a, a, "dcol")
                for t in range(NT):
                    for s in range(NT):
                        last = pe.matmul(bank[:, 2 * t:2 * t + 2], inc_t[:, s, c(t)], w_hl[:, s, :],
                                         start=s == 0, stop=s == NT - 1)
                last.then_inc(ring_a.fill("dcol"), 1)

            def to_nodes(a, _):
                for t in range(DT):
                    bank = take(ring_a, a, f"g{t}")
                    for s in range(NT):
                        if t == 0:
                            pe.wait_ge(m_hi_ready.sem, m_hi_ready.at(a, s + 1))
                            pe.wait_ge(m_lo_ready.sem, m_lo_ready.at(a, s + 1))
                        pe.matmul(bank[:], m_hi[:, s, c(t)], inc_t[:, s, :], start=s == 0, stop=False)
                        last = pe.matmul(bank[:], m_lo[:, s, c(t)], inc_t[:, s, :], start=False, stop=s == NT - 1)
                    last.then_inc(ring_a.fill(f"g{t}"), 1)
                    if t == 0:
                        pe.wait_ge(dn_rep_ready.sem, dn_rep_ready.at(a, 1))
                        bank = take(ring_a, a, "drow")
                        for s in range(NT):
                            last = pe.transpose(bank[:, c(s)], dn_rep[:, s, :], ident[:])
                        last.then_inc(ring_a.fill("drow"), 1)

            def hidden(a, t):
                bank = take(ring_a, a, f"h{t}")
                for s in range(DT):
                    if t == 0:
                        pe.wait_ge(g_hi_ready.sem, g_hi_ready.at(a, s + 1))
                        pe.wait_ge(g_lo_ready.sem, g_lo_ready.at(a, s + 1))
                    last = add_products(bank, w1t_hi[:, s, c(t)], w1t_lo[:, s, c(t)], g_hi[:, s, :], g_lo[:, s, :],
                                        C, C, s == 0, s == DT - 1)
                last.then_inc(ring_a.fill(f"h{t}"), 1)

            def project(a, _):
                for s in range(HT_):
                    pe.wait_ge(h_hi_ready.sem, h_hi_ready.at(a, s + 1))
                    pe.wait_ge(h_lo_ready.sem, h_lo_ready.at(a, s + 1))
                    settle(pe, "tensor")
                    for t in range(NT):
                        bank = take(ring_a, a, f"z{t}") if s == 0 else ring_a.bank(f"z{t}")
                        add_products(bank, h_hi[:, s, c(t)], h_lo[:, s, c(t)], w2c_hi[:, s, :], w2c_lo[:, s, :],
                                     D + 2, D, s == 0, s == HT_ - 1)
                pe.wait_ge(sq_summed.sem, sq_summed.at(a, 3))
                for t in range(NT):
                    bank = ring_a.bank(f"z{t}")
                    pe.matmul(bank[:, D + 4:D + 5], squares[:, 0, c(t)], ones[:, 0:1], start=False, stop=True,
                              skip_group_check=True).then_inc(ring_a.fill(f"z{t}"), 1)

            def to_edges2(a, s):
                pe.wait_ge(z_hi_ready.sem, z_hi_ready.at(a, s + 1))
                pe.wait_ge(z_lo_ready.sem, z_lo_ready.at(a, s + 1))
                settle(pe, "tensor")
                for t in range(NT):
                    bank = take(ring_a, a, f"n{t}") if s == 0 else ring_a.bank(f"n{t}")
                    pe.matmul(bank[:, 0:D], inc[:, s, c(t)], z_hi[:, s, :], start=s == 0, stop=False)
                    last = pe.matmul(bank[:, 0:D], inc[:, s, c(t)], z_lo[:, s, :], start=False, stop=s == NT - 1)
                    if s == NT - 1:
                        last.then_inc(ring_a.fill(f"n{t}"), 1)

            def to_nodes2(a, _):
                for t in range(NT):
                    bank = take(ring_a, a, f"y{t}")
                    for s in range(NT):
                        if t == 0:
                            pe.wait_ge(m_hi_ready.sem, m_hi_ready.at(a, NT + s + 1))
                            pe.wait_ge(m_lo_ready.sem, m_lo_ready.at(a, NT + s + 1))
                        pe.matmul(bank[:, 0:D], inc_t[:, s, c(t)], m_hi[:, s, :], start=s == 0, stop=False)
                        last = pe.matmul(bank[:, 0:D], inc_t[:, s, c(t)], m_lo[:, s, :], start=False, stop=s == NT - 1)
                    last.then_inc(ring_a.fill(f"y{t}"), 1)

            def x1_t(a, _):
                for t in range(DT):
                    bank = take(ring_a, a, f"xt{t}")
                    for s in range(NT):
                        if t == 0:
                            pe.wait_ge(x1_ready.sem, x1_ready.at(a, s + 1))
                        last = pe.transpose(bank[:, c(s)], x1[:, s, c(t)], ident[:])
                    last.then_inc(ring_a.fill(f"xt{t}"), 1)

            def qk(a, _):
                for name, hi, lo in (("q", wqt_hi, wqt_lo), ("k", wkt_hi, wkt_lo)):
                    for t in range(DT):
                        bank = take(ring_a, a, f"{name}{t}")
                        for s in range(DT):
                            if name == "q" and t == 0:
                                pe.wait_ge(x1t_hi_ready.sem, x1t_hi_ready.at(a, s + 1))
                                pe.wait_ge(x1t_lo_ready.sem, x1t_lo_ready.at(a, s + 1))
                            last = add_products(bank, hi[:, s, c(t)], lo[:, s, c(t)], x1t_hi[:, s, :], x1t_lo[:, s, :],
                                                C, C, s == 0, s == DT - 1)
                        last.then_inc(ring_a.fill(f"{name}{t}"), 1)

            def make_values(a, _):
                for t in range(NT):
                    bank = take(ring_a, a, f"v{t}")
                    last = split_products(bank, [(x1t_hi[:, s, c(t)], x1t_lo[:, s, c(t)], wvt_hi[:, s, :], wvt_lo[:, s, :])
                                                 for s in range(DT)], D, D)
                    last.then_inc(ring_a.fill(f"v{t}"), 1)

            def attend(a, i):
                for kind, n in attention_parts(i, TILES):
                    name = f"{kind}{n}"
                    if kind == "s":
                        row, head = divmod(n, HEADS)
                        if n < GROUP:
                            pe.wait_ge(packed[n].sem, packed[n].at(a, packed[n].per))
                        bank = take(ring_a, a, name)
                        pe.matmul(bank[:], q_pack[0:PACKED, head, c(row)], k_pack[0:PACKED, head, :], start=True,
                                  stop=True).then_inc(ring_a.fill(name), 1)
                    elif kind == "t":
                        pe.wait_ge(probs_ready.sem, probs_ready.at(a, n + 1))
                        bank = take(ring_a, a, name)
                        for s in range(NT):
                            last = pe.transpose(bank[:, c(s)], probs[:, n % P_RING, c(s)], ident[:])
                        last.then_inc(ring_a.fill(name), 1)
                    elif kind == "r":
                        pe.wait_ge(rrep_ready.sem, rrep_ready.at(a, n + 1))
                        bank = take(ring_a, a, name)
                        pe.transpose(bank[:, 0:P], recip_rep[:, n % 2, :], ident[:]).then_inc(ring_a.fill(name), 1)
                    elif kind[0] == "c":
                        s = int(kind[1])
                        if s == 0:
                            both_pt_done(pe, a, GROUP * n + GROUP - 1)
                            if n == 0:
                                pe.wait_ge(values_ready.sem, values_ready.at(a, 4))
                            take(ring_a, a, f"c{n}")
                        bank = ring_a.bank(f"c{n}")
                        for h in range(GROUP):
                            head = (n % 2) * GROUP + h
                            rows = slice(h * HEAD_DIM, (h + 1) * HEAD_DIM)
                            last = pe.matmul(bank[rows, 0:P], values[:, s, head * HEAD_DIM:(head + 1) * HEAD_DIM],
                                             probs_t[:, (GROUP * n + h) % PT_RING, s, :],
                                             start=s == 0, stop=s == NT - 1)
                        if s == NT - 1:
                            last.then_inc(ring_a.fill(f"c{n}"), 1)
                    elif kind == "at":
                        bank = take(ring_a, a, name)
                        for s in range(NT):
                            last = pe.transpose(bank[:, c(s)], mask[:, s, c(n)], ident[:])
                        last.then_inc(ring_a.fill(name), 1)
                    else:
                        pe.wait_ge(cx_hi_ready.sem, cx_hi_ready.at(a, 2 * n + 2))
                        pe.wait_ge(cx_lo_ready.sem, cx_lo_ready.at(a, 2 * n + 2))
                        bank = take(ring_a, a, name)
                        last = split_products(bank, [(cx_hi[:, s, :], cx_lo[:, s, :], wot_hi[:, s, :], wot_lo[:, s, :])
                                                     for s in range(DT)], D, D)
                        last.then_inc(ring_a.fill(name), 1)



            def x2_t(b, _):
                pe.wait_ge(x2_ready.sem, x2_ready.at(b, 4))
                for t in range(DT):
                    bank = take(ring_b, b, f"xt{t}")
                    for s in range(NT):
                        last = pe.transpose(bank[:, c(s)], x2[:, s, c(t)], ident[:])
                    last.then_inc(ring_b.fill(f"xt{t}"), 1)

            def linear(b, t):
                if t == 0:
                    pe.wait_ge(xt_hi_ready.sem, xt_hi_ready.at(b, 2))
                    pe.wait_ge(xt_lo_ready.sem, xt_lo_ready.at(b, 2))
                    settle(pe, "tensor")
                bank = take(ring_b, b, f"l{t}")
                last = split_products(bank, [(xt_hi[:, s, c(t)], xt_lo[:, s, c(t)], l2t_hi[:, s, :], l2t_lo[:, s, :])
                                             for s in range(DT)], 2 * D, 2 * D)
                last.then_inc(ring_b.fill(f"l{t}"), 1)

            def spread(b, name, t, r_hi, r_lo, wide):
                bank = take(ring_b, b, f"{name}{t}")
                last = split_products(bank, [(adjt_hi[:, s, c(t)], adjt_lo[:, s, c(t)], r_hi[:, s, :], r_lo[:, s, :])
                                             for s in range(NT)], wide, D)
                last.then_inc(ring_b.fill(f"{name}{t}"), 1)

            def aggregate(b, t):
                if t == 0:
                    pe.wait_ge(adjt_hi_ready.sem, adjt_hi_ready.at(b, 4))
                    pe.wait_ge(adjt_lo_ready.sem, adjt_lo_ready.at(b, 4))
                    pe.wait_ge(y_hi_ready.sem, y_hi_ready.at(b, 4))
                    pe.wait_ge(y_lo_ready.sem, y_lo_ready.at(b, 4))
                spread(b, "n", t, y_hi, y_lo, D + 2)

            def x3_t(b, _):
                pe.wait_ge(x3_ready.sem, x3_ready.at(b, 4))
                for t in range(DT):
                    bank = take(ring_b, b, f"x3t{t}")
                    for s in range(NT):
                        last = pe.transpose(bank[:, c(s)], x3[:, s, c(t)], ident[:])
                    last.then_inc(ring_b.fill(f"x3t{t}"), 1)

            def mix(b, t):
                if t == 0:
                    pe.wait_ge(xt_hi_ready.sem, xt_hi_ready.at(b, 4))
                    pe.wait_ge(xt_lo_ready.sem, xt_lo_ready.at(b, 4))
                    settle(pe, "tensor")
                for name, lo_col, hi_col in ((f"ya{t}", 0, 2 * D), (f"yb{t}", 2 * D, MIX + 2)):
                    bank = take(ring_b, b, name)
                    w = hi_col - lo_col
                    last = split_products(bank, [(xt_hi[:, s, c(t)], xt_lo[:, s, c(t)], mix_hi[:, s, lo_col:hi_col],
                                                  mix_lo[:, s, lo_col:hi_col]) for s in range(DT)], w, w)
                    last.then_inc(ring_b.fill(name), 1)

            def source(b, _):
                bank = take(ring_b, b, "si")
                last = split_products(bank, [(urep_hi[:, s, :], urep_lo[:, s, :], xt_hi[:, s, :], xt_lo[:, s, :])
                                             for s in range(DT)], C, C)
                last.then_inc(ring_b.fill("si"), 1)

            def hop1(b, t):
                if t == 0:
                    pe.wait_ge(adjt_hi_ready.sem, adjt_hi_ready.at(b, 8))
                    pe.wait_ge(adjt_lo_ready.sem, adjt_lo_ready.at(b, 8))
                    pe.wait_ge(y_hi_ready.sem, y_hi_ready.at(b, 8))
                    pe.wait_ge(y_lo_ready.sem, y_lo_ready.at(b, 8))
                    settle(pe, "tensor")
                spread(b, "u", t, y_hi, y_lo, D + 2)

            def hop2(b, t):
                if t == 0:
                    pe.wait_ge(v_hi_ready.sem, v_hi_ready.at(b, 4))
                    pe.wait_ge(v_lo_ready.sem, v_lo_ready.at(b, 4))
                spread(b, "w", t, v_hi, v_lo, D)

            drive(pe, {("A", "incidence"): incidence, ("A", "to_edges"): to_edges, ("A", "degrees"): degrees,
                       ("A", "to_nodes"): to_nodes, ("A", "hidden"): hidden, ("A", "project"): project,
                       ("A", "to_edges2"): to_edges2, ("A", "to_nodes2"): to_nodes2, ("A", "x1_t"): x1_t,
                       ("A", "qk"): qk, ("A", "values"): make_values, ("A", "attend"): attend, ("B", "attend"): attend,
                       ("B", "x2_t"): x2_t, ("B", "linear"): linear,
                       ("B", "aggregate"): aggregate, ("B", "x3_t"): x3_t, ("B", "mix"): mix,
                       ("B", "source"): source, ("B", "hop1"): hop1, ("B", "hop2"): hop2})

        @block.scalar
        def _(act):
            copy = ACT.Copy

            def split_x(a, _):
                act.wait_ge(x_loaded.sem, x_loaded.at(a, 16))
                act_a.link(act, act.activation(x_hi[:, :, D:D + 2], ones[:, :].rearrange("p (a b) -> p a b", b=2), copy))
                act.activation(x_hi[:, :, 0:D], x_in[:], copy).then_inc(x_hi_ready.sem, 1)

            def to_edges(a, t):
                act.wait_ge(ring_a.fill(f"m{t}"), ring_a.full(a, f"m{t}"))
                bank = ring_a.bank(f"m{t}")
                act.wait_ge(be_ready.sem, be_ready.at(a, t + 1))
                act.activation(m_hi[:, t, :], bank[:, 0:D], copy, scale=be[:, t:t + 1]).then_inc(m_hi_ready.sem, 1)

            def to_nodes(a, _):
                act.wait_ge(ring_a.fill("drow"), ring_a.full(a, "drow"))
                act.activation(dn_row[:], ring_a.bank("drow")[:], copy).then_inc(drow_ready.sem, 1)
                for t in range(DT):
                    act.wait_ge(g_ready.sem, g_ready.at(a, t + 1))
                    act.activation(g_hi[:, t, :], tmp_a[:, t, :], copy).then_inc(g_hi_ready.sem, 1)

            def hidden(a, t):
                act.wait_ge(ring_a.fill(f"h{t}"), ring_a.full(a, f"h{t}"))
                bank = ring_a.bank(f"h{t}")
                if t >= 2:
                    act.wait_ge(h_hi_ready.sem, h_hi_ready.at(a, t - 1))
                    act.wait_ge(h_lo_ready.sem, h_lo_ready.at(a, t - 1))
                else:
                    act.wait_ge(g_lo_ready.sem, g_lo_ready.at(a, 2))
                act.activation(tmp_a[:, t % 2, :], bank[:], ACT.Relu, bias=b1_col[:, t:t + 1]).then_inc(h_ready.sem, 1)
                act.wait_ge(h_ready.sem, h_ready.at(a, t + 1))
                act.activation(squares[:, t, :], tmp_a[:, t % 2, :], ACT.Square).then_inc(sq_ready.sem, 1)

            def rescale(a, _):
                for t in range(NT):
                    act.wait_ge(z_ready.sem, z_ready.at(a, t + 1))
                    act.activation(z_hi[:, t, :], tmp_a[:, t % 2, 0:D], copy).then_inc(z_hi_ready.sem, 1)

            def to_edges2(a, t):
                act.wait_ge(ring_a.fill(f"n{t}"), ring_a.full(a, f"n{t}"))
                bank = ring_a.bank(f"n{t}")
                act.activation(m_hi[:, t, :], bank[:, 0:D], copy, scale=be[:, t:t + 1]).then_inc(m_hi_ready.sem, 1)

            def x1_t(a, _):
                for t in range(DT):
                    act.wait_ge(ring_a.fill(f"xt{t}"), ring_a.full(a, f"xt{t}"))
                    bank = ring_a.bank(f"xt{t}")
                    act.activation(x1t_hi[:, t, :], bank[:], copy).then_inc(x1t_hi_ready.sem, 1)

            def qk(a, _):
                for name, dst, bias in (("q", q_hi, bq_col), ("k", k_hi, bk_col)):
                    for t in range(DT):
                        act.wait_ge(ring_a.fill(f"{name}{t}"), ring_a.full(a, f"{name}{t}"))
                        bank = ring_a.bank(f"{name}{t}")
                        act.activation(dst[:, t, :], bank[:], ACT.Identity, bias=bias[:, t:t + 1])\
                           .then_inc(qk_hi_ready.sem, 1)

            def attend(a, i):
                if 1 <= i <= TILES:
                    j = i - 1
                    act.wait_ge(top_ready.sem, top_ready.at(a, j + 1))
                    act.activation(probs[:, j % P_RING, :], probs[:, j % P_RING, :], ACT.Exp, bias=neg_top[:, j:j + 1],
                                   scale=SCALE2, accum_out=sums[:, j:j + 1]).then_inc(probs_ready.sem, 1)
                for kind, n in attention_parts(i, TILES):
                    if kind == "t" and n in on_scalar:
                        act.wait_ge(ring_a.fill(f"t{n}"), ring_a.full(a, f"t{n}"))
                        bank = ring_a.bank(f"t{n}")
                        act.activation(probs_t[:, n % PT_RING, :, :], bank[:].rearrange("p (s q) -> p s q", s=NT),
                                       copy).then_inc(pt_scalar.sem, 1)
                    if kind == "at":
                        act.wait_ge(ring_a.fill(f"at{n}"), ring_a.full(a, f"at{n}"))
                        act.activation(adjt_hi[:, n, :], ring_a.bank(f"at{n}")[:], copy).then_inc(adjt_hi_ready.sem, 1)
                n = every(i, 9, GROUP, TILES // GROUP)
                if n is not None:
                    act.wait_ge(ring_a.fill(f"r{n}"), ring_a.full(a, f"r{n}"))
                    act.activation(recip_t[:, n % 2, :], ring_a.bank(f"r{n}")[:, 0:P], copy).then_inc(rt_ready.sem, 1)
                n = every(i, 13, GROUP, TILES // GROUP)
                if n is not None:
                    act.wait_ge(cx_ready.sem, cx_ready.at(a, n + 1))
                    act.activation(cx_hi[:, n % 2, :], cx_tmp[:, n % 2, :], copy).then_inc(cx_hi_ready.sem, 1)



            def turned(b, names, n):
                for t in range(DT):
                    act.wait_ge(ring_b.fill(f"{names}{t}"), ring_b.full(b, f"{names}{t}"))
                    bank = ring_b.bank(f"{names}{t}")
                    act.activation(xt_hi[:, t, :], bank[:], copy).then_inc(xt_hi_ready.sem, 1)

            def linear(b, t):
                act.wait_ge(ring_b.fill(f"l{t}"), ring_b.full(b, f"l{t}"))
                bank = ring_b.bank(f"l{t}")
                if t == 0:
                    act.wait_ge(stored.sem, stored.at(b, 16))
                act.activation(y_hi[:, t, 0:D], bank[:, D:2 * D], copy).then_inc(y_hi_ready.sem, 1)
                act.activation(y01[:, t, 0:D], bank[:, 0:D], copy).then_inc(y01_ready.sem, 1)

            def mix(b, t):
                act.wait_ge(ring_b.fill(f"ya{t}"), ring_b.full(b, f"ya{t}"))
                bank = ring_b.bank(f"ya{t}")
                act.activation(y01[:, t, D:2 * D], bank[:, D:2 * D], copy).then_inc(y01_ready.sem, 1)
                act.wait_ge(ring_b.fill(f"yb{t}"), ring_b.full(b, f"yb{t}"))
                bank = ring_b.bank(f"yb{t}")
                act.activation(y_hi[:, t, 0:D], bank[:, 0:D], copy).then_inc(y_hi_ready.sem, 1)

            def source(b, _):
                act.wait_ge(ring_b.fill("si"), ring_b.full(b, "si"))
                bank = ring_b.bank("si")
                act.activation(si_row[:], bank[:], copy).then_inc(si_ready.sem, 1)

            def alpha_exp(b, t):
                if t < 2:
                    act.wait_ge(sj_ready.sem, sj_ready.at(b, 4))
                    act.wait_ge(si_ready.sem, si_ready.at(b, 1))
                else:
                    act.wait_ge(alpha_ready.sem, alpha_ready.at(b, t - 1))
                act.activation(e_tmp[:, t % 2, :], si_row[:], ACT.Exp, bias=sj_col[:, t:t + 1])
                act.activation(e_small[:, t % 2, :], si_row[:], ACT.Exp, bias=sj_small[:, t:t + 1], scale=LEAK)\
                   .then_inc(exp_ready.sem, 1)

            def alpha_split(b, t):
                act.wait_ge(alpha_ready.sem, alpha_ready.at(b, t + 1))
                act.activation(adjt_hi[:, t, :], alpha_whole[:, t, :], copy).then_inc(adjt_hi_ready.sem, 1)

            def hop1(b, t):
                act.wait_ge(v_ready.sem, v_ready.at(b, t + 1))
                act.activation(v_hi[:, t, :], v_tmp[:, t % 2, :], copy).then_inc(v_hi_ready.sem, 1)

            drive(act, {("A", "split_x"): split_x, ("A", "to_edges"): to_edges, ("A", "to_nodes"): to_nodes,
                        ("A", "hidden"): hidden, ("A", "rescale"): rescale, ("A", "to_edges2"): to_edges2,
                        ("A", "x1_t"): x1_t, ("A", "qk"): qk, ("A", "attend"): attend, ("B", "attend"): attend,
                        ("B", "x2_split"): lambda b, n: turned(b, "xt", 0),
                        ("B", "linear_out"): linear, ("B", "x3_split"): lambda b, n: turned(b, "x3t", 2),
                        ("B", "mix_out"): mix, ("B", "source_out"): source, ("B", "alpha_exp"): alpha_exp,
                        ("B", "alpha_split"): alpha_split, ("B", "hop1_out"): hop1},
                  chains["act"])

        @block.gpsimd
        def _(pool):
            def minus(dst, src, hi):
                return pool.tensor_tensor(dst, src, plain(hi), ALU.subtract)

            def split_x(a, _):
                pool.wait_ge(x_hi_ready.sem, x_hi_ready.at(a, 1))
                minus(x_lo[:], x_in[:], x_hi[:, :, 0:D]).then_inc(x_lo_ready.sem, 1)
            def residual0(a, _):
                pool.wait_ge(x_lo_ready.sem, x_lo_ready.at(a, 1))
                pool_a.link(pool, pool.tensor_tensor(x_in[:], x_in[:], x_in[:], ALU.add))
                for t in range(NT):
                    last = pool.tensor_tensor(x_in[:, t, :], x_in[:, t, :], b2_row[:], ALU.add)
                last.then_inc(x2b_ready.sem, 1)



            def hidden(a, t):
                pool.wait_ge(h_hi_ready.sem, h_hi_ready.at(a, t + 1))
                minus(h_lo[:, t, :], tmp_a[:, t % 2, :], h_hi[:, t, :]).then_inc(h_lo_ready.sem, 1)

            def inverse_root(dst, src, n):
                return pool.tensor_tensor(dst, src, half_neg[:, 0:n], ALU.pow)

            def project(a, _):
                pool.wait_ge(var_ready.sem, var_ready.at(a, 1))
                settle(pool, "pool")
                inverse_root(stat[:, 4, :], stat[:, 3, :], NT).then_inc(rstd_ready.sem, 1)

            def rescale(a, _):
                for t in range(NT):
                    pool.wait_ge(z_hi_ready.sem, z_hi_ready.at(a, t + 1))
                    settle(pool, "pool")
                    minus(z_lo[:, t, :], tmp_a[:, t % 2, 0:D], z_hi[:, t, :]).then_inc(z_lo_ready.sem, 1)

            def to_nodes2(a, _):
                pool.wait_ge(var_ready.sem, var_ready.at(a, 2))
                inverse_root(rs_a[:], ve_a[:], NT).then_inc(rstd_ready.sem, 1)

            def attend(a, i):
                if i == 1:
                    pool.wait_ge(x1t_lo_ready.sem, x1t_lo_ready.at(a, 2))
                    for t in range(NT):
                        last = pool.tensor_tensor(x1[:, t, :], x1[:, t, :], bo_row[:], ALU.add)
                    last.then_inc(x1b_ready.sem, 1)
                n = every(i, 13, GROUP, TILES // GROUP)
                if n is not None:
                    pool.wait_ge(cx_hi_ready.sem, cx_hi_ready.at(a, n + 1))
                    minus(cx_lo[:, n % 2, :], cx_tmp[:, n % 2, :], cx_hi[:, n % 2, :]).then_inc(cx_lo_ready.sem, 1)
                n = every(i, 21, HEADS, NT)
                if n is not None:
                    pool.wait_ge(var_ready.sem, var_ready.at(a, 3 + n))
                    inverse_root(rs_a[:, n:n + 1], ve_a[:, n:n + 1], 1).then_inc(rstd_ready.sem, 1)

            def norm2(b, _):
                pool.wait_ge(var_b.sem, var_b.at(b, 1))
                inverse_root(rs_b[:], ve_b[:], NT).then_inc(rstd_b.sem, 1)

            def merge(b, t):
                if t == 0:
                    pool.wait_ge(n_read.sem, n_read.at(b, 4))
                pool.tensor_tensor(adj_whole[:, t, :], plain(adjt_hi[:, t, :]), plain(adjt_lo[:, t, :]), ALU.add)\
                    .then_inc(merged.sem, 1)

            def alpha_exp(b, t):
                if t == 0:
                    pool.wait_ge(merged.sem, merged.at(b, 4))
                pool.wait_ge(lrelu_ready.sem, lrelu_ready.at(b, t + 1))
                pool.tensor_tensor(alpha_whole[:, t, :], adj_whole[:, t, :], e_tmp[:, t % 2, :], ALU.mult)\
                    .then_inc(alpha_ready.sem, 1)

            def hop1(b, t):
                pool.wait_ge(v_hi_ready.sem, v_hi_ready.at(b, t + 1))
                minus(v_lo[:, t, :], v_tmp[:, t % 2, :], v_hi[:, t, :]).then_inc(v_lo_ready.sem, 1)

            def norm3(b, _):
                pool.wait_ge(var_b.sem, var_b.at(b, 2))
                inverse_root(rs_b[:], ve_b[:], NT).then_inc(rstd_b.sem, 1)

            drive(pool, {("A", "split_x"): split_x, ("A", "residual0"): residual0, ("A", "hidden"): hidden,
                         ("A", "project"): project, ("A", "rescale"): rescale, ("A", "to_nodes2"): to_nodes2,
                         ("A", "attend"): attend, ("B", "attend"): attend, ("B", "norm2"): norm2, ("B", "merge"): merge,
                         ("B", "alpha_exp"): alpha_exp,
                         ("B", "hop1_out"): hop1, ("B", "norm3"): norm3}, chains["pool"])

        @block.vector
        def _(dve):
            dve.sem_inc(stored.sem, 16)

            def link_a(ins):
                chain_a.link(dve, ins)

            def link_b(ins):
                chain_b.link(dve, ins)

            def low(dst, src, hi):
                return dve.tensor_tensor(dst, src, plain(hi), ALU.subtract)



            def normal(dst, src, mv, rs, t):
                return dve.tensor_scalar(dst, src, mv[:, t, 0:1], rs[:, t:t + 1], ALU.subtract, ALU.mult)

            def inc_rows(a, t):
                dve.wait_ge(adj_in[t].sem, adj_in[t].at(a, 16))
                dve.tensor_scalar(inc[:, t, :], mask[:, t, :], 0.0, None, ALU.not_equal).then_inc(inc_ready.sem, 1)

            def incidence(a, _):
                for t in range(NT):
                    dve.wait_ge(ring_a.fill(f"ht{t}"), ring_a.full(a, f"ht{t}"))
                    bank = ring_a.bank(f"ht{t}")
                    dve.tensor_copy(w_col[:, t:t + 1], bank[:, 0:1])
                    dve.tensor_scalar(inc_t[:, t, :], bank[:], 0.0, None, ALU.not_equal).then_inc(inc_t_ready.sem, 1)
                dve.wait_ge(inc_t_ready.sem, inc_t_ready.at(a, NT))
                link_a(dve.tensor_copy(w_hl[:, :, 0], w_col[:]))
                low(w_hl[:, :, 1], w_col[:], w_hl[:, :, 0]).then_inc(w_ready.sem, 1)

            def to_edges(a, t):
                dve.wait_ge(ring_a.fill(f"m{t}"), ring_a.full(a, f"m{t}"))
                bank = ring_a.bank(f"m{t}")
                link_a(dve.tensor_scalar(be_t[:, t:t + 1], bank[:, D:D + 1], 0.5, None, ALU.max))
                dve.reciprocal(be[:, t:t + 1], be_t[:, t:t + 1]).then_inc(be_ready.sem, 1)
                dve.wait_ge(m_hi_ready.sem, m_hi_ready.at(a, t + 1))
                dve.scalar_tensor_tensor(out=m_lo[:, t, :], in0=bank[:, 0:D], scalar=be[:, t:t + 1],
                                         in1=plain(m_hi[:, t, :]), op0=ALU.mult, op1=ALU.subtract)\
                   .then_inc(m_lo_ready.sem, 1)

            def degrees(a, _):
                dve.wait_ge(ring_a.fill("dcol"), ring_a.full(a, "dcol"))
                bank = ring_a.bank("dcol")
                pair = bank[:, 0:2 * NT].rearrange("p (t k) -> p t k", k=2)
                link_a(dve.tensor_copy(dn_t[:, 0, :], pair[:, :, 0]))
                dve.tensor_tensor(dn_t[:, 0, :], pair[:, :, 1], dn_t[:, 0, :], ALU.add).then_inc(dcol_read.sem, 1)
                dve.wait_ge(dcol_read.sem, dcol_read.at(a, 1))
                link_a(dve.tensor_scalar(dn_t[:, 1, :], dn_t[:, 0, :], TINY, None, ALU.max))
                link_a(dve.reciprocal(dn_t[:, 1, :], dn_t[:, 1, :]))
                link_a(dve.scalar_tensor_tensor(out=dn[:], in0=dn_t[:, 0, :], scalar=0.0, in1=dn_t[:, 1, :],
                                                op0=ALU.is_gt, op1=ALU.mult))
                dve.tensor_copy(dn_rep[:], dn[:].rearrange("p (t o) -> p t o", o=1).to_broadcast([P, NT, P]))\
                   .then_inc(dn_rep_ready.sem, 1)

            def to_nodes(a, _):
                dve.wait_ge(drow_ready.sem, drow_ready.at(a, 1))
                for t in range(DT):
                    dve.wait_ge(ring_a.fill(f"g{t}"), ring_a.full(a, f"g{t}"))
                    bank = ring_a.bank(f"g{t}")
                    dve.tensor_tensor(tmp_a[:, t, :], bank[:], dn_row[:], ALU.mult).then_inc(g_ready.sem, 1)
                for t in range(DT):
                    dve.wait_ge(g_hi_ready.sem, g_hi_ready.at(a, t + 1))
                    low(g_lo[:, t, :], tmp_a[:, t, :], g_hi[:, t, :]).then_inc(g_lo_ready.sem, 1)

            def sum_squares(a, t):
                dve.wait_ge(sq_ready.sem, sq_ready.at(a, t + 1))
                if t >= 2:
                    dve.wait_ge(sq_summed.sem, sq_summed.at(a, t - 1))
                dve.tensor_tensor(squares[:, 0, :], squares[:, 0, :], squares[:, t, :], ALU.add).then_inc(sq_summed.sem, 1)

            def hidden(a, t):
                dve.wait_ge(h_ready.sem, h_ready.at(a, t + 1))
                dve.tensor_copy(h_hi[:, t, :], tmp_a[:, t % 2, :]).then_inc(h_hi_ready.sem, 1)
                if t >= 2:
                    sum_squares(a, t - 1)
                if t == HT_ - 1:
                    sum_squares(a, t)

            def project(a, _):
                for t in range(NT):
                    dve.wait_ge(ring_a.fill(f"z{t}"), ring_a.full(a, f"z{t}"))
                    bank = ring_a.bank(f"z{t}")
                    link_a(dve.tensor_scalar(stat[:, 0, t:t + 1], bank[:, D:D + 1], 1.0 / DH, None, ALU.mult))
                    link_a(dve.tensor_scalar(stat[:, 1, t:t + 1], bank[:, D + 4:D + 5], 1.0 / DH, None, ALU.mult))
                link_a(dve.tensor_tensor(stat[:, 2, :], stat[:, 0, :], stat[:, 0, :], ALU.mult))
                link_a(dve.tensor_tensor(stat[:, 3, :], stat[:, 1, :], stat[:, 2, :], ALU.subtract))
                dve.tensor_scalar(stat[:, 3, :], stat[:, 3, :], 0.0, LN_EPS, ALU.max, ALU.add).then_inc(var_ready.sem, 1)

            def rescale(a, _):
                dve.wait_ge(rstd_ready.sem, rstd_ready.at(a, 1))
                for t in range(NT):
                    bank = ring_a.bank(f"z{t}")
                    if t >= 2:
                        dve.wait_ge(z_lo_ready.sem, z_lo_ready.at(a, t - 1))
                    dve.scalar_tensor_tensor(out=tmp_a[:, t % 2, 0:D], in0=bank[:, 0:D], scalar=stat[:, 4, t:t + 1],
                                             in1=betaw2_row[:], op0=ALU.mult, op1=ALU.add).then_inc(z_ready.sem, 1)

            def to_edges2(a, t):
                dve.wait_ge(ring_a.fill(f"n{t}"), ring_a.full(a, f"n{t}"))
                bank = ring_a.bank(f"n{t}")
                dve.wait_ge(m_hi_ready.sem, m_hi_ready.at(a, NT + t + 1))
                dve.scalar_tensor_tensor(out=m_lo[:, t, :], in0=bank[:, 0:D], scalar=be[:, t:t + 1],
                                         in1=plain(m_hi[:, t, :]), op0=ALU.mult, op1=ALU.subtract)\
                   .then_inc(m_lo_ready.sem, 1)

            def to_nodes2(a, _):
                dve.wait_ge(x2b_ready.sem, x2b_ready.at(a, 1))
                for t in range(NT + 2):
                    if t < NT:
                        dve.wait_ge(ring_a.fill(f"y{t}"), ring_a.full(a, f"y{t}"))
                        bank = ring_a.bank(f"y{t}")
                        dve.scalar_tensor_tensor(out=x1[:, t, :], in0=bank[:, 0:D], scalar=dn[:, t:t + 1],
                                                 in1=x_in[:, t, :], op0=ALU.mult, op1=ALU.add).then_inc(y_read.sem, 1)
                    if 0 <= t - 1 < NT:
                        dve.wait_ge(y_read.sem, y_read.at(a, t))
                        settle(dve, "vector")
                        dve.bn_stats(bn_a[:, t - 1, :], x1[:, t - 1, :]).then_inc(y_stats.sem, 1)
                    if t >= 2:
                        dve.wait_ge(y_stats.sem, y_stats.at(a, t - 1))
                        settle(dve, "vector")
                        dve.bn_aggr(mv_a[:, t - 2, :], bn_a[:, t - 2, :]).then_inc(y_moments.sem, 1)
                dve.wait_ge(y_moments.sem, y_moments.at(a, NT))
                dve.tensor_scalar(ve_a[:], mv_a[:, :, 1], LN_EPS, None, ALU.add).then_inc(var_ready.sem, 1)

            def normal1(a, _):
                dve.wait_ge(rstd_ready.sem, rstd_ready.at(a, 2))
                for t in range(NT):
                    normal(x1[:, t, :], x1[:, t, :], mv_a, rs_a, t).then_inc(x1_ready.sem, 1)

            def x1_t(a, _):
                for t in range(DT):
                    bank = ring_a.bank(f"xt{t}")
                    dve.wait_ge(x1t_hi_ready.sem, x1t_hi_ready.at(a, t + 1))
                    low(x1t_lo[:, t, :], bank[:], x1t_hi[:, t, :]).then_inc(x1t_lo_ready.sem, 1)

            def qk(a, _):
                for n, (name, hi, lo, bias) in enumerate((("q", q_hi, q_lo, bq_col), ("k", k_hi, k_lo, bk_col))):
                    for t in range(DT):
                        bank = ring_a.bank(f"{name}{t}")
                        dve.wait_ge(qk_hi_ready.sem, qk_hi_ready.at(a, 2 * n + t + 1))
                        dve.scalar_tensor_tensor(out=lo[:, t, :], in0=bank[:], scalar=bias[:, t:t + 1],
                                                 in1=plain(hi[:, t, :]), op0=ALU.add, op1=ALU.subtract)\
                           .then_inc(qk_lo_ready.sem, 1)

            def make_values(a, _):
                for t in range(NT):
                    dve.wait_ge(ring_a.fill(f"v{t}"), ring_a.full(a, f"v{t}"))
                    bank = ring_a.bank(f"v{t}")
                    dve.tensor_tensor(values[:, t, :], bank[:, 0:D], bv_row[:], ALU.add).then_inc(values_ready.sem, 1)

            def attend(a, i):
                if i < TILES:
                    dve.wait_ge(ring_a.fill(f"s{i}"), ring_a.full(a, f"s{i}"))
                    bank = ring_a.bank(f"s{i}")
                    settle(dve, "vector")
                    dve.tensor_tensor_reduce(probs[:, i % P_RING, :], bank[:], mask[:, i // HEADS, :], 1.0, -3.4e38,
                                             ALU.mult, ALU.max, top[:, i:i + 1]).then_inc(masked.sem, 1)
                if 1 <= i <= TILES:
                    dve.wait_ge(masked.sem, masked.at(a, i))
                    dve.tensor_scalar(neg_top[:, i - 1:i], top[:, i - 1:i], -SCALE2, None, ALU.mult)\
                       .then_inc(top_ready.sem, 1)
                n = every(i, 12, GROUP, TILES // GROUP)
                if n is not None:
                    dve.wait_ge(rt_ready.sem, rt_ready.at(a, n + 1))
                    dve.wait_ge(ring_a.fill(f"c{n}"), ring_a.full(a, f"c{n}"))
                    dve.tensor_tensor(cx_tmp[:, n % 2, :], ring_a.bank(f"c{n}")[:, 0:P], recip_t[:, n % 2, :], ALU.mult)\
                       .then_inc(cx_ready.sem, 1)
                if i - 1 in AT_STEPS:
                    n = AT_STEPS.index(i - 1)
                    dve.wait_ge(adjt_hi_ready.sem, adjt_hi_ready.at(a, n + 1))
                    low(adjt_lo[:, n, :], ring_a.bank(f"at{n}")[:], adjt_hi[:, n, :]).then_inc(adjt_lo_ready.sem, 1)
                n = every(i, 19, HEADS, NT)
                if n is not None:
                    if n == 0:
                        dve.wait_ge(x1b_ready.sem, x1b_ready.at(a, 1))
                    dve.wait_ge(ring_a.fill(f"o{n}"), ring_a.full(a, f"o{n}"))
                    bank = ring_a.bank(f"o{n}")
                    dve.tensor_tensor(x2[:, n, :], bank[:, 0:D], x1[:, n, :], ALU.add).then_inc(o_read.sem, 1)
                for kind, n in attention_parts(i, TILES):
                    if kind == "t" and n in on_vector:
                        dve.wait_ge(ring_a.fill(f"t{n}"), ring_a.full(a, f"t{n}"))
                        bank = ring_a.bank(f"t{n}")
                        dve.tensor_copy(probs_t[:, n % PT_RING, :, :], bank[:].rearrange("p (s q) -> p s q", s=NT))\
                           .then_inc(pt_vector.sem, 1)



                n = every(i, 20, HEADS, NT)
                if n is not None:
                    dve.wait_ge(o_read.sem, o_read.at(a, n + 1))
                    settle(dve, "vector")
                    dve.bn_stats(bn_a[:, n, :], x2[:, n, :]).then_inc(o_stats.sem, 1)
                n = every(i, 21, HEADS, NT)
                if n is not None:
                    dve.wait_ge(o_stats.sem, o_stats.at(a, n + 1))
                    settle(dve, "vector")
                    dve.bn_aggr(mv_a[:, n, :], bn_a[:, n, :]).then_inc(o_moments.sem, 1)
                    dve.wait_ge(o_moments.sem, o_moments.at(a, n + 1))
                    dve.tensor_scalar(ve_a[:, n:n + 1], mv_a[:, n, 1:2], LN_EPS, None, ALU.add).then_inc(var_ready.sem, 1)
                n = every(i, 23, HEADS, NT)
                if n is not None:
                    dve.wait_ge(rstd_ready.sem, rstd_ready.at(a, 3 + n))
                    normal(x2[:, n, :], x2[:, n, :], mv_a, rs_a, n).then_inc(x2_ready.sem, 1)
                n = every(i, 6, GROUP, TILES // GROUP)
                if n is not None:
                    dve.wait_ge(probs_ready.sem, probs_ready.at(a, GROUP * n + GROUP))
                    four = slice(GROUP * n, GROUP * n + GROUP)
                    dve.reciprocal(rsum[:, four], sums[:, four]).then_inc(rsum_ready.sem, 1)
                n = every(i, 7, GROUP, TILES // GROUP)
                if n is not None:
                    dve.wait_ge(rsum_ready.sem, rsum_ready.at(a, n + 1))
                    four = slice(GROUP * n, GROUP * n + GROUP)
                    dve.tensor_copy(recip_rep[:, n % 2, :].rearrange("p (h d) -> p h d", h=GROUP),
                                    rsum[:, four].rearrange("p (h o) -> p h o", o=1).to_broadcast([P, GROUP, HEAD_DIM]))\
                       .then_inc(rrep_ready.sem, 1)



            def turned(b, names, n):
                for t in range(DT):
                    dve.wait_ge(xt_hi_ready.sem, xt_hi_ready.at(b, n + t + 1))
                    low(xt_lo[:, t, :], ring_b.bank(f"{names}{t}")[:], xt_hi[:, t, :]).then_inc(xt_lo_ready.sem, 1)

            def linear(b, t):
                dve.wait_ge(y_hi_ready.sem, y_hi_ready.at(b, t + 1))
                dve.wait_ge(y01_ready.sem, y01_ready.at(b, t + 1))
                low(y_lo[:, t, :], ring_b.bank(f"l{t}")[:, D:2 * D], y_hi[:, t, 0:D]).then_inc(y_lo_ready.sem, 1)

            def aggregate(b, t):
                dve.wait_ge(ring_b.fill(f"n{t}"), ring_b.full(b, f"n{t}"))
                bank = ring_b.bank(f"n{t}")
                link_b(dve.tensor_scalar(bdeg[:, 0, t:t + 1], bank[:, D:D + 1], DEG_EPS, None, ALU.max))
                link_b(dve.reciprocal(bdeg[:, 1, t:t + 1], bdeg[:, 0, t:t + 1]))
                dve.scalar_tensor_tensor(out=x3[:, t, :], in0=bank[:, 0:D], scalar=bdeg[:, 1, t:t + 1],
                                         in1=y01[:, t, 0:D], op0=ALU.mult, op1=ALU.add).then_inc(n_read.sem, 1)
                dve.wait_ge(n_read.sem, n_read.at(b, t + 1))
                dve.scalar_tensor_tensor(out=x3[:, t, :], in0=x3[:, t, :], scalar=0.0, in1=x2[:, t, :],
                                         op0=ALU.max, op1=ALU.add).then_inc(x3_sum.sem, 1)

            def moments(b, n, t, src):
                settle(dve, "vector")
                dve.bn_stats(bn_b[:, t, :], src).then_inc(b_stats.sem, 1)
                dve.wait_ge(b_stats.sem, b_stats.at(b, n + t + 1))
                settle(dve, "vector")
                dve.bn_aggr(mv_b[:, t, :], bn_b[:, t, :]).then_inc(b_moments.sem, 1)
                if t == NT - 1:
                    dve.wait_ge(b_moments.sem, b_moments.at(b, n + NT))
                    dve.tensor_scalar(ve_b[:], mv_b[:, :, 1], LN_EPS, None, ALU.add).then_inc(var_b.sem, 1)

            def agg_stats(b, t):
                dve.wait_ge(x3_sum.sem, x3_sum.at(b, t + 1))
                moments(b, 0, t, x3[:, t, :])

            def norm2(b, _):
                dve.wait_ge(rstd_b.sem, rstd_b.at(b, 1))
                for t in range(NT):
                    normal(x3[:, t, :], x3[:, t, :], mv_b, rs_b, t).then_inc(x3_ready.sem, 1)

            def mix(b, t):
                dve.wait_ge(y01_ready.sem, y01_ready.at(b, NT + t + 1))
                dve.tensor_tensor(y01[:, t, 0:D], ring_b.bank(f"ya{t}")[:, 0:D], bm_row[:], ALU.add)\
                   .then_inc(y0_ready.sem, 1)
                dve.wait_ge(y_hi_ready.sem, y_hi_ready.at(b, NT + t + 1))
                bank = ring_b.bank(f"yb{t}")
                dve.tensor_tensor(sj_col[:, t:t + 1], bank[:, D:D + 1], shift_col, ALU.add).then_inc(sj_sum.sem, 1)
                low(y_lo[:, t, :], bank[:, 0:D], y_hi[:, t, 0:D]).then_inc(y_lo_ready.sem, 1)
                dve.wait_ge(sj_sum.sem, sj_sum.at(b, t + 1))
                dve.tensor_scalar(sj_small[:, t:t + 1], sj_col[:, t:t + 1], LEAK, None, ALU.mult).then_inc(sj_ready.sem, 1)

            def alpha_exp(b, t):
                dve.wait_ge(exp_ready.sem, exp_ready.at(b, t + 1))
                dve.tensor_tensor(e_tmp[:, t % 2, :], e_tmp[:, t % 2, :], e_small[:, t % 2, :], ALU.max)\
                   .then_inc(lrelu_ready.sem, 1)

            def alpha_split(b, t):
                dve.wait_ge(adjt_hi_ready.sem, adjt_hi_ready.at(b, NT + t + 1))
                low(adjt_lo[:, t, :], alpha_whole[:, t, :], adjt_hi[:, t, :]).then_inc(adjt_lo_ready.sem, 1)

            def hop1(b, t):
                dve.wait_ge(ring_b.fill(f"u{t}"), ring_b.full(b, f"u{t}"))
                bank = ring_b.bank(f"u{t}")
                link_b(dve.tensor_scalar(bdeg[:, 0, t:t + 1], bank[:, D:D + 1], SUM_EPS, None, ALU.add))
                link_b(dve.reciprocal(bdeg[:, 1, t:t + 1], bdeg[:, 0, t:t + 1]))
                if t >= 2:
                    dve.wait_ge(v_lo_ready.sem, v_lo_ready.at(b, t - 1))
                dve.scalar_tensor_tensor(out=v_tmp[:, t % 2, :], in0=bank[:, 0:D], scalar=bdeg[:, 1, t:t + 1],
                                         in1=y01[:, t, D:2 * D], op0=ALU.mult, op1=ALU.add).then_inc(v_ready.sem, 1)

            def hop2_sum(b, t):
                dve.wait_ge(ring_b.fill(f"w{t}"), ring_b.full(b, f"w{t}"))
                bank = ring_b.bank(f"w{t}")
                dve.wait_ge(y0_ready.sem, y0_ready.at(b, t + 1))
                dve.scalar_tensor_tensor(out=y01[:, t, 0:D], in0=bank[:, 0:D], scalar=bdeg[:, 1, t:t + 1],
                                         in1=y01[:, t, 0:D], op0=ALU.mult, op1=ALU.add).then_inc(w_read.sem, 1)
                dve.wait_ge(w_read.sem, w_read.at(b, t + 1))
                dve.scalar_tensor_tensor(out=y01[:, t, 0:D], in0=y01[:, t, 0:D], scalar=0.0, in1=x3[:, t, :],
                                         op0=ALU.max, op1=ALU.add).then_inc(hop2_done.sem, 1)

            def hop2_stats(b, t):
                dve.wait_ge(hop2_done.sem, hop2_done.at(b, t + 1))
                moments(b, NT, t, y01[:, t, 0:D])

            def norm3(b, _):
                dve.wait_ge(rstd_b.sem, rstd_b.at(b, 2))
                for t in range(NT):
                    last = normal(y01[:, t, 0:D], y01[:, t, 0:D], mv_b, rs_b, t)
                last.then_inc(out_ready.sem, 1)

            drive(dve, {("A", "inc_rows"): inc_rows, ("A", "incidence"): incidence, ("A", "to_edges"): to_edges, ("A", "degrees"): degrees,
                        ("A", "to_nodes"): to_nodes, ("A", "hidden"): hidden, ("A", "project"): project,
                        ("A", "rescale"): rescale, ("A", "normal1"): normal1,
                        ("A", "to_edges2"): to_edges2, ("A", "to_nodes2"): to_nodes2, ("A", "x1_t"): x1_t,
                        ("A", "qk"): qk, ("A", "values"): make_values, ("A", "attend"): attend, ("B", "attend"): attend,
                        ("B", "x2_split"): lambda b, n: turned(b, "xt", 0),
                        ("B", "linear_out"): linear, ("B", "agg_sum"): aggregate, ("B", "agg_stats"): agg_stats,
                        ("B", "norm2"): norm2,
                        ("B", "x3_split"): lambda b, n: turned(b, "x3t", 2), ("B", "mix_out"): mix,
                        ("B", "alpha_exp"): alpha_exp, ("B", "alpha_split"): alpha_split,
                        ("B", "hop1_out"): hop1, ("B", "hop2_sum"): hop2_sum, ("B", "hop2_stats"): hop2_stats,
                        ("B", "norm3"): norm3}, chains["dve"])


_INS = ["x", "adj", "L0_gnn_W1", "L0_gnn_b1", "L0_gnn_gamma", "L0_gnn_beta", "L0_gnn_W2", "L0_gnn_b2", "L1_gnn_Wq",
        "L1_gnn_bq", "L1_gnn_Wk", "L1_gnn_bk", "L1_gnn_Wv", "L1_gnn_bv", "L1_gnn_Wo", "L1_gnn_bo", "L2_gnn_W",
        "L3_gnn_Wv", "L3_gnn_bv", "L3_gnn_aw", "L3_gnn_ab", "L3_gnn_Wk", "L3_gnn_bk"]


def kernel(**inputs):
    import numpy as _np
    import concourse.bacc as _bacc
    from concourse import mybir as _mybir
    from concourse.bass_utils import run_bass_kernel_spmd as _run

    nc = _bacc.Bacc("TRN2", target_bir_lowering=False, num_devices=1)
    arrays, args = {}, []
    for name in _INS:
        a = _np.ascontiguousarray(inputs[name])
        arrays[f"in_{name}_dram"] = a
        args.append(nc.dram_tensor(f"in_{name}_dram", a.shape, _mybir.dt.from_np(a.dtype), kind="ExternalInput").ap())
    shape = tuple(inputs["x"].shape)
    args.append(nc.dram_tensor("out_0_dram", shape, _mybir.dt.from_np(_np.dtype("float32")), kind="ExternalOutput").ap())
    build(nc, *args)
    r = _run(nc, [arrays], core_ids=[0])
    return r.results[0]["out_0_dram"]
```
